# Optimizing a Trainium2 kernel written in Bass

```python
import numpy as np
import jax
import jax.numpy as jnp

def _softmax(x, axis=-1):
    return jax.nn.softmax(x, axis=axis)

def _gelu(x):
    return jax.nn.gelu(x, approximate=True)

def _silu(x):
    return jax.nn.silu(x)

def _sigmoid(x):
    return jax.nn.sigmoid(x)

def _layernorm(x, axis=-1, eps=1e-05):
    m = jnp.mean(x, axis=axis, keepdims=True)
    v = jnp.var(x, axis=axis, keepdims=True)
    return (x - m) / jnp.sqrt(v + eps)

def _scatter_add(tgt, idx, src, axis=0):
    return tgt.at[idx].add(src)

def _segment_sum(src, seg, n):
    return jax.ops.segment_sum(src, seg, n)
kernel_name = 'mk_adaln_attn_ffn_d1_seqx_r4_60e4e9'

def setup_inputs(seed: int=0):
    np.random.seed(seed)
    _w = jnp.asarray

    def _rec_inputs():
        import jax
        import jax.numpy as jnp
        _rk = jax.random.key(seed)
        x = -0.000125 + 0.9999 * jax.random.normal(jax.random.fold_in(_rk, 1), (8, 256, 1024), jnp.float32)
        _lenS = 256 - jax.random.randint(jax.random.fold_in(_rk, 7), (8,), 0, max(1, 256 // 4) + 1, jnp.int32)
        _lenS2 = 256 - jax.random.randint(jax.random.fold_in(_rk, 8), (8,), 0, max(1, 256 // 4) + 1, jnp.int32)
        itok_B_0_7 = jax.random.randint(jax.random.fold_in(_rk, 11), (8,), 0, 8, jnp.int32)
        itok_B_0_23 = jax.random.randint(jax.random.fold_in(_rk, 12), (8,), 0, 24, jnp.int32)
        return (x, itok_B_0_7, itok_B_0_23)
    x, itok_B_0_7, itok_B_0_23 = _rec_inputs()

    def _L0_cond_setup():
        import jax, jax.numpy as jnp
        import numpy as np
        TOP_K = 2
        LANG_BIAS = 5.0
        SCALING = 32.0 / 16.0
        LANGUAGE_PAD_ID = -1
        key = jax.random.key(seed)
        ks = jax.random.split(key, 6)
        B, T, D, O, E, R = (4, 512, 1024, 1024, 8, 16)
        x = jax.random.normal(ks[0], (B, T, D), dtype=jnp.float32)
        language_ids = jax.random.randint(ks[1], (B,), 0, E).astype(jnp.int64)
        W = jax.random.normal(ks[2], (O, D), dtype=jnp.float32) * (1.0 / np.sqrt(D))
        Wr = jax.random.normal(ks[3], (E, D), dtype=jnp.float32) * (1.0 / np.sqrt(D))
        A = jax.random.normal(ks[4], (E, R, D), dtype=jnp.float32) * (1.0 / np.sqrt(D))
        Bm = jax.random.normal(ks[5], (O, R), dtype=jnp.float32) * 0.0
        Bm = jnp.broadcast_to(Bm, (E, O, R)) + jax.random.normal(ks[5], (E, O, R), dtype=jnp.float32) * 0.02
        return {'x': x, 'language_ids': language_ids, 'W': W, 'Wr': Wr, 'A': A, 'B': Bm}
    _L0_cond_all = _L0_cond_setup()
    _L0_cond_in = {k: v for k, v in _L0_cond_all.items() if k in ('W', 'Wr', 'A', 'B')}
    del _L0_cond_all

    def _L0_attn_setup():
        import jax, jax.numpy as jnp
        import numpy as np
        B, S, H = (1, 512, 1024)
        N_HEADS, N_KV, HEAD_DIM = (32, 8, 128)
        ROPE_THETA = 10000.0

        def _rope_tables(seqlen, dim, theta):
            inv_freq = 1.0 / theta ** (jnp.arange(0, dim, 2, dtype=jnp.float32) / dim)
            t = jnp.arange(seqlen, dtype=jnp.float32)
            freqs = jnp.outer(t, inv_freq)
            return (jnp.cos(freqs), jnp.sin(freqs))

        def _apply_rope(x, cos, sin):
            d2 = x.shape[-1] // 2
            x1, x2 = (x[..., :d2], x[..., d2:])
            c = cos[None, :, None, :]
            s = sin[None, :, None, :]
            return jnp.concatenate([x1 * c - x2 * s, x1 * s + x2 * c], axis=-1)
        key = jax.random.key(seed)
        k1, k2, k3 = jax.random.split(key, 3)
        hidden_states = jax.random.normal(k1, (B, S, H), dtype=jnp.float32)
        Wqkv = jax.random.normal(k2, ((N_HEADS + 2 * N_KV) * HEAD_DIM, H), dtype=jnp.float32) * 0.02
        Wo = jax.random.normal(k3, (H, N_HEADS * HEAD_DIM), dtype=jnp.float32) * 0.02
        return {'hidden_states': hidden_states, 'Wqkv': Wqkv, 'Wo': Wo}
    _L0_attn_all = _L0_attn_setup()
    _L0_attn_in = {k: v for k, v in _L0_attn_all.items() if k in ('Wqkv', 'Wo')}
    del _L0_attn_all

    def _L0_cond2_setup():
        import jax, jax.numpy as jnp
        import numpy as np
        R = 16
        ALPHA = 32
        SCALING = ALPHA / R
        SLOTS = 32
        IN_F = 1024
        OUT_F = 1024
        B, T = (8, 256)
        key = jax.random.key(seed)
        k1, k2, k3, k4, k5, k6 = jax.random.split(key, 6)
        x = jax.random.normal(k1, (B, T, IN_F), dtype=jnp.float32)
        adapter_mapping = jax.random.randint(k2, (B,), 0, SLOTS, dtype=jnp.int32)
        W = jax.random.normal(k3, (OUT_F, IN_F), dtype=jnp.float32) * 0.02
        b = jax.random.normal(k4, (OUT_F,), dtype=jnp.float32) * 0.02
        lora_As = jax.random.normal(k5, (SLOTS, IN_F, R), dtype=jnp.float32) * 0.02
        lora_Bs = jax.random.normal(k6, (SLOTS, R, OUT_F), dtype=jnp.float32) * 0.02
        return {'x': x, 'adapter_mapping': adapter_mapping, 'W': W, 'b': b, 'lora_As': lora_As, 'lora_Bs': lora_Bs}
    _L0_cond2_all = _L0_cond2_setup()
    _L0_cond2_in = {k: v for k, v in _L0_cond2_all.items() if k in ('W', 'b', 'lora_As', 'lora_Bs')}
    del _L0_cond2_all

    def _L0_ffn_setup():
        import jax, jax.numpy as jnp
        import numpy as np
        B, S, D, O, E, R = (4, 512, 1024, 1024, 8, 16)
        SCALING = 32.0 / 16.0
        MAX_THRESHOLD = 0.125
        key = jax.random.key(seed)
        ks = jax.random.split(key, 8)
        return {'x': jax.random.normal(ks[0], (B, S, D), jnp.float32), 'W_base': jax.random.normal(ks[1], (O, D), jnp.float32) * (1.0 / np.sqrt(D)), 'b_base': jax.random.normal(ks[2], (O,), jnp.float32) * 0.02, 'W_gate': jax.random.normal(ks[3], (E, D), jnp.float32) * (1.0 / np.sqrt(D)), 'W_thr': jax.random.normal(ks[4], (D,), jnp.float32) * (1.0 / np.sqrt(D)), 'b_thr': jax.random.normal(ks[5], (1,), jnp.float32) * 0.02, 'A_w': jax.random.normal(ks[6], (E, R, D), jnp.float32) * (1.0 / np.sqrt(D)), 'B_w': jax.random.normal(ks[7], (E, O, R), jnp.float32) * (1.0 / np.sqrt(R))}
    _L0_ffn_all = _L0_ffn_setup()
    _L0_ffn_in = {k: v for k, v in _L0_ffn_all.items() if k in ('W_base', 'b_base', 'W_gate', 'W_thr', 'b_thr', 'A_w', 'B_w')}
    del _L0_ffn_all
    return {'x': x, 'itok_B_0_7': itok_B_0_7, 'itok_B_0_23': itok_B_0_23, 'L0_cond_W': _L0_cond_in['W'], 'L0_cond_Wr': _L0_cond_in['Wr'], 'L0_cond_A': _L0_cond_in['A'], 'L0_cond_B': _L0_cond_in['B'], 'L0_attn_Wqkv': _L0_attn_in['Wqkv'], 'L0_attn_Wo': _L0_attn_in['Wo'], 'L0_cond2_W': _L0_cond2_in['W'], 'L0_cond2_b': _L0_cond2_in['b'], 'L0_cond2_lora_As': _L0_cond2_in['lora_As'], 'L0_cond2_lora_Bs': _L0_cond2_in['lora_Bs'], 'L0_ffn_W_base': _L0_ffn_in['W_base'], 'L0_ffn_b_base': _L0_ffn_in['b_base'], 'L0_ffn_W_gate': _L0_ffn_in['W_gate'], 'L0_ffn_W_thr': _L0_ffn_in['W_thr'], 'L0_ffn_b_thr': _L0_ffn_in['b_thr'], 'L0_ffn_A_w': _L0_ffn_in['A_w'], 'L0_ffn_B_w': _L0_ffn_in['B_w']}

def reference(x, itok_B_0_7, itok_B_0_23, L0_cond_W, L0_cond_Wr, L0_cond_A, L0_cond_B, L0_attn_Wqkv, L0_attn_Wo, L0_cond2_W, L0_cond2_b, L0_cond2_lora_As, L0_cond2_lora_Bs, L0_ffn_W_base, L0_ffn_b_base, L0_ffn_W_gate, L0_ffn_W_thr, L0_ffn_b_thr, L0_ffn_A_w, L0_ffn_B_w):
    import jax
    import jax.numpy as jnp

    def _L0_cond_ref(x, language_ids, W, Wr, A, B):
        import jax, jax.numpy as jnp
        import numpy as np
        TOP_K = 2
        LANG_BIAS = 5.0
        SCALING = 32.0 / 16.0
        LANGUAGE_PAD_ID = -1
        base = jnp.einsum('btd,od->bto', x, W)
        E = Wr.shape[0]
        logits = jnp.einsum('btd,ed->bte', x.astype(jnp.float32), Wr.astype(jnp.float32))
        expert_targets = language_ids
        valid = expert_targets >= 0
        tgt = jnp.where(valid, expert_targets, 0)
        bias = jax.nn.one_hot(tgt, E, dtype=logits.dtype) * LANG_BIAS
        bias = jnp.where(valid[:, None], bias, 0.0)
        logits = logits + bias[:, None, :]
        topw, topi = jax.lax.top_k(logits, TOP_K)
        weights = jax.nn.softmax(topw, axis=-1)
        gates = jnp.sum(jax.nn.one_hot(topi, E, dtype=weights.dtype) * weights[..., None], axis=-2)
        gates = gates.astype(x.dtype)
        h = jnp.einsum('btd,erd->bter', x, A)
        lora_out = jnp.einsum('bter,bte,eor->bto', h, gates, B)
        return base + SCALING * lora_out

    def _L0_attn_ref(hidden_states, Wqkv, Wo):
        import jax, jax.numpy as jnp
        import numpy as np
        B, S, H = (1, 512, 1024)
        N_HEADS, N_KV, HEAD_DIM = (32, 8, 128)
        ROPE_THETA = 10000.0

        def _rope_tables(seqlen, dim, theta):
            inv_freq = 1.0 / theta ** (jnp.arange(0, dim, 2, dtype=jnp.float32) / dim)
            t = jnp.arange(seqlen, dtype=jnp.float32)
            freqs = jnp.outer(t, inv_freq)
            return (jnp.cos(freqs), jnp.sin(freqs))

        def _apply_rope(x, cos, sin):
            d2 = x.shape[-1] // 2
            x1, x2 = (x[..., :d2], x[..., d2:])
            c = cos[None, :, None, :]
            s = sin[None, :, None, :]
            return jnp.concatenate([x1 * c - x2 * s, x1 * s + x2 * c], axis=-1)
        b, s, h = hidden_states.shape
        qkv = jnp.einsum('bsh,oh->bso', hidden_states, Wqkv)
        q_end = N_HEADS * HEAD_DIM
        k_end = q_end + N_KV * HEAD_DIM
        xq = qkv[..., :q_end].reshape(b, s, N_HEADS, HEAD_DIM)
        xk = qkv[..., q_end:k_end].reshape(b, s, N_KV, HEAD_DIM)
        xv = qkv[..., k_end:].reshape(b, s, N_KV, HEAD_DIM)
        cos, sin = _rope_tables(s, HEAD_DIM, ROPE_THETA)
        xq = _apply_rope(xq, cos, sin)
        xk = _apply_rope(xk, cos, sin)
        groups = N_HEADS // N_KV
        xk = jnp.repeat(xk, groups, axis=2)
        xv = jnp.repeat(xv, groups, axis=2)
        scale = 1.0 / jnp.sqrt(jnp.float32(HEAD_DIM))
        scores = jnp.einsum('bqhd,bkhd->bhqk', xq, xk) * scale
        causal = jnp.tril(jnp.ones((s, s), dtype=bool))
        scores = jnp.where(causal[None, None, :, :], scores, jnp.float32(-1e+30))
        probs = jax.nn.softmax(scores, axis=-1)
        out = jnp.einsum('bhqk,bkhd->bqhd', probs, xv).reshape(b, s, N_HEADS * HEAD_DIM)
        attn_output = jnp.einsum('bsd,hd->bsh', out, Wo)
        return attn_output

    def _L0_cond2_ref(x, adapter_mapping, W, b, lora_As, lora_Bs):
        import jax, jax.numpy as jnp
        import numpy as np
        R = 16
        ALPHA = 32
        SCALING = ALPHA / R
        SLOTS = 32
        IN_F = 1024
        OUT_F = 1024
        B, T = (8, 256)
        base_out = jnp.einsum('bti,oi->bto', x, W) + b
        A = lora_As[adapter_mapping]
        Bm = lora_Bs[adapter_mapping]
        lora_h = jnp.einsum('bti,bir->btr', x, A)
        lora_out = jnp.einsum('btr,bro->bto', lora_h, Bm)
        return base_out + lora_out * SCALING

    def _L0_ffn_ref(x, W_base, b_base, W_gate, W_thr, b_thr, A_w, B_w):
        import jax, jax.numpy as jnp
        import numpy as np
        B, S, D, O, E, R = (4, 512, 1024, 1024, 8, 16)
        SCALING = 32.0 / 16.0
        MAX_THRESHOLD = 0.125
        base = jnp.einsum('bsd,od->bso', x, W_base) + b_base
        xf = x.reshape(-1, D)
        gate = jax.nn.softmax(xf @ W_gate.T, axis=-1)
        thr = jax.nn.sigmoid(xf @ W_thr + b_thr[0]) * MAX_THRESHOLD
        adapted = gate - thr[:, None]
        selected = (adapted >= 0).astype(x.dtype)
        w = adapted * selected
        wsum = jnp.sum(w, axis=-1, keepdims=True)
        wsum = jnp.where(wsum == 0, jnp.ones_like(wsum), wsum)
        w = w / wsum
        h = jnp.einsum('nd,erd->ner', xf, A_w)
        moe = jnp.einsum('ner,ne,eor->no', h, w, B_w) * SCALING
        return base + moe.reshape(base.shape)
    x = x + _L0_attn_ref(_L0_cond_ref(x, itok_B_0_7, L0_cond_W, L0_cond_Wr, L0_cond_A, L0_cond_B), L0_attn_Wqkv, L0_attn_Wo)
    x = x + _L0_ffn_ref(_L0_cond2_ref(x, itok_B_0_23, L0_cond2_W, L0_cond2_b, L0_cond2_lora_As, L0_cond2_lora_Bs), L0_ffn_W_base, L0_ffn_b_base, L0_ffn_W_gate, L0_ffn_W_thr, L0_ffn_b_thr, L0_ffn_A_w, L0_ffn_B_w)
    return x

_drawn_inputs = setup_inputs


def setup_inputs(seed=0):
    import zlib

    import numpy as np

    out = dict(_drawn_inputs(seed))
    spreads = {}
    factors = {'L0_cond_Wr': 8.0, 'L0_ffn_b_base': 3.893}
    for name, (base, spread) in spreads.items():
        noise = np.random.default_rng([zlib.crc32(name.encode()), seed]).standard_normal(out[name].shape)
        drawn = base * np.exp(spread * noise) if base else spread * noise
        out[name] = jnp.asarray(drawn.astype(out[name].dtype))
    for name, factor in factors.items():
        out[name] = (out[name] * factor).astype(out[name].dtype)
    return out
```

```python
from contextlib import ExitStack

import numpy as np
import concourse.bass as bass
from concourse import mybir

F32 = mybir.dt.float32
F32R = mybir.dt.float32r
I32 = mybir.dt.int32
ALU = mybir.AluOpType
ACT = mybir.ActivationFunctionType
AX = mybir.AxisListType.X

P = 128
SAMPLES, SEQ, D = 8, 256, 1024
KT = D // P
CHUNK = 512
CHUNKS = SAMPLES * SEQ // CHUNK
CS = CHUNK // SEQ
TT = CHUNK // P
HEADS, KV, HD = 32, 8, 128
HG = HEADS // KV
QT = SEQ // P
E, R = 8, 16
SLOTS = 32
SCALE = float(1.0 / np.sqrt(np.float32(HD)))
MASKED = -1e30
LANG_BIAS = 5.0
LORA_SCALE = 2.0
MAX_THRESHOLD = 0.125

RING = 5
TILES = {"pre": 16, "body": 10, "post": 24}
BODIES = KV - 1
TILES_CHUNK = TILES["pre"] + BODIES * TILES["body"] + TILES["post"]
GATHER_AT = 90
assert TILES_CHUNK % RING == 0 and TILES["body"] % RING == 0 and GATHER_AT % RING == 0

COUNTS = {
    "mm_ready":   (14, 14, 24, 1),
    "mm_hi":      (8, 0, 8, 0),
    "mm_read":    (14, 14, 24, 2),
    "s_ready":    (2, 8, 9, 0),
    "s_read":     (2, 8, 9, 1),
    "ptb_ready":  (3, 7, 8, 0),
    "ptb_hi":     (1, 7, 6, 0),
    "ptb_read":   (3, 7, 8, 1),
    "o_ready":    (0, 4, 6, 0),
    "o_hi":       (0, 4, 4, 0),
    "o_read":     (0, 4, 6, 2),
    "nmax_ready": (0, 4, 4, 0),
    "exp_ready":  (0, 4, 4, 0),
    "rsum_ready": (0, 4, 4, 0),
    "p_ready":    (0, 4, 4, 0),
    "xs_ready":   (5, 5, 0, 0),
    "t2_ready":   (5, 5, 0, 0),
    "rope_sum":   (5, 5, 0, 0),
    "rope_hi":    (5, 5, 0, 0),
    "rope_lo":    (5, 5, 0, 1),
    "x_hi":       (8, 0, 0, 0),
    "x_lo":       (8, 0, 0, 0),
    "x1_hi":      (0, 0, 8, 0),
    "x1_lo":      (0, 0, 8, 0),
    "shift_ready": (1, 0, 1, 0),
    "gate_exp":   (1, 0, 1, 0),
    "gate_step":  (11, 0, 14, 0),
    "gates_ready": (1, 0, 1, 0),
    "hg_hi":      (1, 0, 2, 0),
    "hg_lo":      (1, 0, 2, 0),
}

C_COS, C_SIN, C_MASK, C_ID, C_TRI, C_IOTA, C_OWN = 0, 256, 512, 768, 896, 960, 968
C_COLS = C_OWN + SAMPLES
B_2, B_B, B_THR = 0, KT, 2 * KT
WG_STEP = 16
WG_COLS = (KT - 1) * WG_STEP + P


class Section:

    def __init__(self, kind, c, g=0):
        self.kind, self.c, self.g = kind, c, g

    def count(self, pre, body, post, k):
        per_chunk = pre + BODIES * body + post
        if self.kind == "pre":
            return self.c * per_chunk + k
        if self.kind == "body":
            return self.c * per_chunk + self.g * body + (pre + k)
        return self.c * per_chunk + (pre + BODIES * body + k)

    def value(self, name, k):
        pre, body, post, at_start = COUNTS[name]
        return self.count(pre, body, post, k + at_start)

    def slot(self, tile):
        before = {"pre": 0, "body": TILES["pre"], "post": TILES["pre"] + BODIES * TILES["body"]}[self.kind]
        return (before + tile) % RING

    def round(self, tile):
        before = {"pre": 0, "body": TILES["pre"], "post": TILES["pre"] + BODIES * TILES["body"]}[self.kind]
        turns = (before + tile) // RING + 1
        per_chunk, per_body = TILES_CHUNK // RING, TILES["body"] // RING
        if self.kind == "body":
            return self.c * per_chunk + self.g * per_body + turns
        return self.c * per_chunk + turns


def build(nc, x_in, stream, adapters_a, adapters_b, gate_w, consts, biases, ids, out):
    ctx = ExitStack()
    with ctx:
        def sb(name, shape, dt=F32):
            return ctx.enter_context(nc.sbuf_tensor(name, shape, dt))

        def psum(name, shape):
            return ctx.enter_context(nc.psum_tensor(name, shape, F32))

        gathered_a = nc.dram_tensor("gathered_a", (P, KT, SAMPLES, R), F32, kind="Internal").ap()
        gathered_b = nc.dram_tensor("gathered_b", (SAMPLES, R, D), F32, kind="Internal").ap()

        hid = sb("hid", [P, 2, KT, CHUNK], F32R)
        wide = sb("wide", [P, 4, HG, CHUNK], F32R)
        acc = sb("acc", [P, KT, CHUNK])
        k_t = sb("k_t", [P, 2, CHUNK], F32R)
        v_tok = sb("v_tok", [P, 2, TT, HD], F32R)
        v_raw = sb("v_raw", [P, CHUNK])
        probs = sb("probs", [P, CS, QT, HG, SEQ])
        p_t = sb("p_t", [P, 2, 2, CHUNK], F32R)
        w_raw_sb = sb("w_raw_sb", [P, RING, D])
        w_sb = sb("w_sb", [P, RING, 2, D], F32R)
        lora_b = sb("lora_b", [P, 2, D], F32R)
        swap = sb("swap", [P, 2, CHUNK])
        turn = sb("turn", [P, 2, CHUNK])
        gw_raw = sb("gw_raw", [P, 2, WG_COLS])
        gw = sb("gw", [P, 2, 2, WG_COLS], F32R)
        cst = sb("cst", [P, C_COLS])
        bia = sb("bia", [P, 2 * KT + 1])
        neg_bthr = sb("neg_bthr", [P, 1])
        ids_raw = sb("ids_raw", [P, 2, SAMPLES], I32)
        ids_f = sb("ids_f", [P, 2, SAMPLES])
        slot_neg = sb("slot_neg", [P, SAMPLES])
        slot_ids = sb("slot_ids", [P, SAMPLES], I32)
        lang_bias = sb("lang_bias", [P, SAMPLES, E])
        rmax = sb("rmax", [P, 4, HG])
        nmax = sb("nmax", [P, 4, HG])
        rowsum = sb("rowsum", [P, 4, HG])
        rsum = sb("rsum", [P, 4, HG])

        scratch = probs[:].rearrange("p a b c d -> p (a b c d)")
        logits_t = scratch[:, 0:512]
        gates_t = scratch[:, 512:1024]
        hg = scratch[:, 1024:1536]
        gates_rep = scratch[:, 1536:2048]
        beats = scratch[:, 2048:2304]
        ties = scratch[:, 2304:2560]
        small = scratch[:, 2560:2560 + 16 * 40]
        lg = small[:, 0:36]
        shifted = small[:, 40:72]
        expd = small[:, 80:112]
        rank = small[:, 120:152]
        chosen = small[:, 160:192]
        wts = small[:, 200:232]
        gate = small[:, 240:272]
        top = small[:, 280:284]
        wsum = small[:, 320:324]
        winv = small[:, 360:364]
        thr_e = small[:, 400:404]
        thr_1 = small[:, 440:444]
        thr_r = small[:, 480:484]
        thr = small[:, 520:524]
        is_zero = small[:, 560:564]
        wsum1 = small[:, 600:604]

        mm = psum("mm", [P, 2, 512])
        sc = psum("sc", [P, 2, 512])
        ptb = psum("ptb", [P, 512])
        ob = psum("ob", [P, 2, 512])

        def semaphore(name):
            return ctx.enter_context(nc.semaphore(name))

        mm_ready = semaphore("mm_ready")
        mm_hi = semaphore("mm_hi")
        mm_read = semaphore("mm_read")
        s_ready = semaphore("s_ready")
        s_read = semaphore("s_read")
        ptb_ready = semaphore("ptb_ready")
        ptb_hi = semaphore("ptb_hi")
        ptb_read = semaphore("ptb_read")
        o_ready = semaphore("o_ready")
        o_hi = semaphore("o_hi")
        o_read = semaphore("o_read")
        nmax_ready = semaphore("nmax_ready")
        exp_ready = semaphore("exp_ready")
        rsum_ready = semaphore("rsum_ready")
        p_ready = semaphore("p_ready")
        xs_ready = semaphore("xs_ready")
        t2_ready = semaphore("t2_ready")
        rope_sum = semaphore("rope_sum")
        rope_hi = semaphore("rope_hi")
        rope_lo = semaphore("rope_lo")
        x_hi = semaphore("x_hi")
        x_lo = semaphore("x_lo")
        x1_hi = semaphore("x1_hi")
        x1_lo = semaphore("x1_lo")
        shift_ready = semaphore("shift_ready")
        gate_exp = semaphore("gate_exp")
        gate_step = semaphore("gate_step")
        gates_ready = semaphore("gates_ready")
        hg_hi = semaphore("hg_hi")
        hg_lo = semaphore("hg_lo")
        w_raw = [semaphore(f"w_raw{s}") for s in range(RING)]
        w_hi = [semaphore(f"w_hi{s}") for s in range(RING)]
        w_lo = [semaphore(f"w_lo{s}") for s in range(RING)]
        x_loaded = [semaphore(f"x_loaded{k}") for k in range(KT)]
        out_stored = semaphore("out_stored")
        const_loaded = semaphore("const_loaded")
        slots_ready = semaphore("slots_ready")
        adapters_ready = semaphore("adapters_ready")
        gw_hi = semaphore("gw_hi")
        gw_lo = semaphore("gw_lo")
        setup = semaphore("setup")
        passed = semaphore("passed")
        N_CONST = 4

        def f(ap):
            return ap.bitcast(F32)

        cos = cst[:, None, C_COS:C_COS + SEQ].to_broadcast([P, CS, SEQ])
        sin = cst[:, None, C_SIN:C_SIN + SEQ].to_broadcast([P, CS, SEQ])
        ident = cst[:, C_ID:C_ID + P]

        def by_sample(ap):
            return ap.rearrange("p (s t) -> p s t", s=CS)

        def xy(hl, kt):
            return wide[:, 2 * hl + kt // HG, kt % HG, :]

        def q_t(hl, h):
            return wide[:, hl, h, :]

        def o_t(hl, h):
            return wide[:, 2 + hl, h, :]

        block = ctx.enter_context(nc.Block())

        @block.sync
        def _(sp):
            sp.dma_start(ids_raw[:], ids).then_inc(const_loaded, 16)
            sp.dma_start(cst[:], consts).then_inc(const_loaded, 16)
            sp.dma_start(gw_raw[:], gate_w).then_inc(const_loaded, 16)
            sp.dma_start(bia[:], biases).then_inc(const_loaded, 16)
            for t in range(RING):
                sp.dma_start(w_raw_sb[:, t, :], stream[t]).then_inc(w_raw[t], 16)
            sp.wait_ge(slots_ready, 1)
            for b in range(SAMPLES):
                a = sp.value_load(slot_ids[0:1, b:b + 1], min_val=0, max_val=SLOTS - 1)
                sp.dma_start(gathered_a[:, :, b, :], adapters_a[bass.ds(a, 1)].rearrange("s p k r -> p (s k) r")
                             ).then_inc(adapters_ready, 16)
                sp.dma_start(gathered_b[b], adapters_b[bass.ds(a, 1)].rearrange("s r d -> (s r) d")
                             ).then_inc(adapters_ready, 16)
            sp.wait_ge(adapters_ready, 16 * 2 * SAMPLES)
            rounds = TILES_CHUNK // RING

            def load(c, i, s, src):
                sp.wait_ge(w_lo[s], c * rounds + i)
                sp.dma_start(w_raw_sb[:, s, :], src).then_inc(w_raw[s], 16)

            def tile_of_stream(n):
                return stream[bass.ds(n, 1)].rearrange("n p d -> (n p) d")

            with sp.Fori(0, CHUNKS) as c:
                with sp.Fori(1, GATHER_AT // RING) as i:
                    for s in range(RING):
                        load(c, i, s, tile_of_stream(i * RING + s))
                load(c, GATHER_AT // RING, 0, gathered_a.rearrange("p k b r -> p (k b r)"))
                load(c, GATHER_AT // RING, 1, gathered_b.rearrange("b r d -> (b r) d"))
                for s in range(2, RING):
                    load(c, GATHER_AT // RING, s, stream[GATHER_AT + s - 2])
                with sp.Fori(GATHER_AT // RING + 1, rounds) as i:
                    for s in range(RING):
                        load(c, i, s, tile_of_stream(i * RING + (s - 2)))
                for s in range(RING):
                    load(c, rounds, s, stream[s])
            for s in range(RING):
                sp.wait_ge(w_raw[s], 16 * (CHUNKS * rounds + 1))

        @block.tensor
        def _(pe):
            pe.sem_inc(mm_ready, COUNTS["mm_ready"][3])
            pe.sem_inc(mm_read, COUNTS["mm_read"][3])
            pe.sem_inc(s_read, COUNTS["s_read"][3])
            pe.sem_inc(ptb_read, COUNTS["ptb_read"][3])
            pe.sem_inc(o_read, COUNTS["o_read"][3])
            pe.sem_inc(rope_lo, COUNTS["rope_lo"][3])

            def product(bank, w_hi_ap, w_lo_ap, x_hi_ap, x_lo_ap, start, stop):
                nc.tensor.matmul(bank, w_hi_ap, x_hi_ap, start=start, stop=False, skip_group_check=True)
                nc.tensor.matmul(bank, w_hi_ap, x_lo_ap, start=False, stop=False, skip_group_check=True)
                return nc.tensor.matmul(bank, w_lo_ap, x_hi_ap, start=False, stop=stop, skip_group_check=True)

            def tile_ready(sec, tile):
                pe.wait_ge(w_lo[sec.slot(tile)], sec.round(tile))

            def column(slot, hl, n):
                return w_sb[:, slot, hl, n * P:(n + 1) * P]

            def linear(sec, bank, tile, src, kts=range(KT), stop=True, ready=None):
                slot = sec.slot(tile)
                if kts[0] == 0:
                    tile_ready(sec, tile)
                for kt in kts:
                    if ready:
                        ready(kt)
                    last = product(bank, column(slot, 0, kt), column(slot, 1, kt), src(0, kt), src(1, kt),
                                   kt == 0, stop and kt == KT - 1)
                return last

            def hid_src(hl, kt):
                return hid[:, hl, kt, :]

            def logits(sec, which, bank, src, ready):
                for kt in range(KT):
                    ready(kt)
                    cols = slice(kt * WG_STEP, kt * WG_STEP + P)
                    last = product(bank, gw[:, which, 0, cols], gw[:, which, 1, cols], src(0, kt), src(1, kt),
                                   kt == 0, kt == KT - 1)
                last.then_inc(s_ready, 1)

            def lora(sec, bank, i, n):
                product(bank, lora_b[:, 0, i * P:(i + 1) * P], lora_b[:, 1, i * P:(i + 1) * P],
                        p_t[:, 0, 0, :], p_t[:, 0, 1, :], False, True).then_inc(mm_ready, 1)

            def turn_logits(sec, rows, read_k, ordinal):
                pe.wait_ge(s_read, sec.value("s_read", read_k))
                pe.wait_ge(ptb_read, sec.value("ptb_read", ordinal))
                pe.sem_inc(passed, 1)
                for t in range(TT):
                    last = nc.tensor.transpose(ptb[:, t * rows:(t + 1) * rows], logits_t[0:rows, t * P:(t + 1) * P],
                                               cst[0:rows, C_ID:C_ID + rows])
                last.then_inc(ptb_ready, 1)

            def turn_gates(sec, ordinal):
                pe.wait_ge(gates_ready, sec.value("gates_ready", 1))
                pe.wait_ge(ptb_read, sec.value("ptb_read", ordinal))
                for t in range(TT):
                    last = nc.tensor.transpose(ptb[:, t * P:(t + 1) * P], gates_rep[:, t * P:(t + 1) * P], ident)
                last.then_inc(ptb_ready, 1)

            def scores(sec):
                pe.wait_ge(rope_lo, sec.value("rope_lo", 0))
                for n in range(2 * CS * QT):
                    b, qt, pair = n // 4, n // 2 % 2, n % 2
                    pe.wait_ge(s_read, sec.value("s_read", n - 1))
                    for j in range(2):
                        h = 2 * pair + j
                        q0 = b * SEQ + qt * P
                        last = product(sc[:, n % 2, j * SEQ:(j + 1) * SEQ],
                                       q_t(0, h)[:, q0:q0 + P], q_t(1, h)[:, q0:q0 + P],
                                       k_t[:, 0, b * SEQ:(b + 1) * SEQ], k_t[:, 1, b * SEQ:(b + 1) * SEQ], True, True)
                    last.then_inc(s_ready, 1)

            BLOCKS = [(0, 0), (0, 1), (1, 1)]

            def turn_probs(sec, i):
                b, (kt, qt) = i // 3, BLOCKS[i % 3]
                pe.wait_ge(p_ready, sec.value("p_ready", b * QT + qt + 1))
                pe.wait_ge(ptb_read, sec.value("ptb_read", i))
                for h in range(HG):
                    last = nc.tensor.transpose(ptb[:, h * P:(h + 1) * P], probs[:, b, qt, h, kt * P:(kt + 1) * P],
                                               ident)
                last.then_inc(ptb_ready, 1)

            def attend(sec, i):
                b, (kt, qt) = i // 3, BLOCKS[i % 3]
                pe.wait_ge(ptb_read, sec.value("ptb_read", i + 1))
                if kt == 0:
                    pe.wait_ge(o_read, sec.value("o_read", b * QT + qt - 1))
                last = product(ob[:, qt, :], v_tok[:, 0, b * QT + kt, :], v_tok[:, 1, b * QT + kt, :],
                               p_t[:, i % 2, 0, :], p_t[:, i % 2, 1, :], kt == 0, kt == qt)
                if kt == qt:
                    last.then_inc(o_ready, 1)

            def turn_v(sec, out_n, ordinal):
                pe.wait_ge(mm_read, sec.value("mm_read", out_n + 1))
                pe.wait_ge(ptb_read, sec.value("ptb_read", ordinal))
                for t in range(TT):
                    last = nc.tensor.transpose(ptb[:, t * P:(t + 1) * P], v_raw[:, t * P:(t + 1) * P], ident)
                last.then_inc(ptb_ready, 1)

            def bank_free(sec, n):
                pe.wait_ge(mm_read, sec.value("mm_read", n - 1))

            def qkv(sec, i, half, first_out, first_tile, ready=None):
                n = first_out + i
                if half == 0:
                    bank_free(sec, n)
                kts = range(half * KT // 2, (half + 1) * KT // 2)
                last = linear(sec, mm[:, n % 2, :], first_tile + i, hid_src, kts, ready=ready)
                if half == 1:
                    last.then_inc(mm_ready, 1)

            def project(sec, i, first_out, first_tile):
                n, tile = first_out + i, first_tile + i // 2
                if i == 0:
                    pe.wait_ge(o_read, sec.value("o_read", 4))
                if i % 2 == 0:
                    tile_ready(sec, tile)
                bank_free(sec, n)
                slot = sec.slot(tile)
                for h in range(HG):
                    col = (i % 2) * HG + h
                    last = product(mm[:, n % 2, :], column(slot, 0, col), column(slot, 1, col), o_t(0, h), o_t(1, h),
                                   h == 0, h == HG - 1)
                last.then_inc(mm_ready, 1)

            def base_and_lora(sec, first_out, first_tile, b_tile, src, hg_k, between=None):
                for i in range(KT):
                    n = first_out + i
                    bank = mm[:, n % 2, :]
                    bank_free(sec, n)
                    if i == 1 and between:
                        linear(sec, bank, first_tile + i, src, range(0, KT // 2), stop=False)
                        between()
                        linear(sec, bank, first_tile + i, src, range(KT // 2, KT), stop=False)
                    else:
                        linear(sec, bank, first_tile + i, src, stop=False)
                    if i == 1:
                        pe.wait_ge(hg_lo, sec.value("hg_lo", hg_k))
                        tile_ready(sec, b_tile)
                        lora(sec, mm[:, (n - 1) % 2, :], 0, n - 1)
                    if i >= 1:
                        lora(sec, bank, i, n)

            def cond(sec):
                pe.wait_ge(gw_lo, 1)
                pe.wait_ge(s_read, sec.value("s_read", 0))
                logits(sec, 0, sc[:, 0, :], xy, lambda kt: pe.wait_ge(x_lo, sec.value("x_lo", kt + 1)))
                linear(sec, sc[:, 1, :], 0, xy).then_inc(s_ready, 1)
                turn_logits(sec, E, 1, 0)
                base_and_lora(sec, 0, 2, 1, xy, 1, lambda: turn_gates(sec, 1))

            def hid_ready(sec, kt):
                pe.wait_ge(mm_read, sec.value("mm_read", kt + 1))

            def first_group(sec):
                for i in range(6):
                    for half in range(2):
                        qkv(sec, i, half, 8, 10, (lambda kt: hid_ready(sec, kt)) if i == 0 else None)
                        if (i, half) == (3, 0):
                            turn_v(sec, 9, 2)

            def body(sec):
                scores(sec)
                for step in range(12):
                    qkv(sec, step // 2, step % 2, 0, 0)
                    if 2 <= step <= 7:
                        attend(sec, step - 2)
                    if 1 <= step <= 6:
                        turn_probs(sec, step - 1)
                    if step == 8:
                        turn_v(sec, 1, 6)
                for i in range(KT):
                    project(sec, i, 6, 6)

            def last_group(sec):
                scores(sec)
                for i in range(7):
                    if i >= 1:
                        attend(sec, i - 1)
                    if i < 6:
                        turn_probs(sec, i)
                for i in range(KT):
                    project(sec, i, 0, 0)

            def cond2(sec):
                pe.wait_ge(o_read, sec.value("o_read", 3))
                linear(sec, ob[:, 0, :], 4, hid_src,
                       ready=lambda kt: pe.wait_ge(x1_lo, sec.value("x1_lo", kt + 1))).then_inc(o_ready, 1)
                base_and_lora(sec, 8, 6, 5, hid_src, 1)

            def ffn(sec):
                pe.wait_ge(s_read, sec.value("s_read", 7))
                logits(sec, 1, sc[:, 0, :], xy, lambda kt: pe.wait_ge(mm_read, sec.value("mm_read", 8 + kt + 1)))
                pe.wait_ge(o_read, sec.value("o_read", 4))
                linear(sec, ob[:, 1, :], 14, xy).then_inc(o_ready, 1)
                turn_logits(sec, E + 1, 9, 6)
                base_and_lora(sec, 16, 16, 15, xy, 2, lambda: turn_gates(sec, 7))

            with pe.Fori(0, CHUNKS) as c:
                pre = Section("pre", c)
                cond(pre)
                first_group(pre)
                with pe.Fori(0, BODIES) as g:
                    body(Section("body", c, g))
                post = Section("post", c)
                last_group(post)
                cond2(post)
                ffn(post)

        @block.scalar
        def _(act):
            def split_hi(sec, tile, dst=None):
                s = sec.slot(tile)
                act.wait_ge(w_raw[s], sec.round(tile) * 16)
                nc.scalar.copy(w_sb[:, s, 0, :] if dst is None else dst, w_raw_sb[:, s, :]).then_inc(w_hi[s], 1)

            def rope_swap(sec, n, k):
                s = n % 2
                act.wait_ge(mm_ready, sec.value("mm_ready", n + 1))
                act.wait_ge(rope_lo, sec.value("rope_lo", (0, 1, 0, 2, 3)[k]))
                nc.scalar.copy(swap[0:P // 2, s, :], mm[P // 2:P, s, :])
                nc.scalar.copy(swap[P // 2:P, s, :], mm[0:P // 2, s, :]).then_inc(xs_ready, 1)

            def write_rope_hi(sec, s, k):
                act.wait_ge(rope_sum, sec.value("rope_sum", k + 1))
                dst = k_t[:, 0, :] if k == 0 else q_t(0, k - 1)
                nc.scalar.copy(dst, turn[:, s, :]).then_inc(rope_hi, 1)

            def probs_hi(sec, i):
                act.wait_ge(ptb_ready, sec.value("ptb_ready", i + 1))
                nc.scalar.copy(p_t[:, i % 2, 0, :], ptb[:]).then_inc(ptb_hi, 1)

            def v_hi(sec, ordinal, k):
                act.wait_ge(ptb_ready, sec.value("ptb_ready", ordinal + 1))
                nc.scalar.copy(v_tok[:, 0, :, :], ptb[:].rearrange("p (t d) -> p t d", t=TT)).then_inc(ptb_hi, 1)

            def write_o_hi(sec, n):
                b, qt = n // QT, n % QT
                act.wait_ge(o_ready, sec.value("o_ready", n + 1))
                t0 = b * SEQ + qt * P
                nc.scalar.copy(wide[:, 2, :, t0:t0 + P], ob[:, qt, :].rearrange("p (h t) -> p h t", h=HG)
                               ).then_inc(o_hi, 1)

            def softmax_exp(sec):
                for n in range(CS * QT):
                    b, qt = n // QT, n % QT
                    keys = (qt + 1) * P
                    act.wait_ge(nmax_ready, sec.value("nmax_ready", n + 1))
                    for h in range(HG):
                        pr = probs[:, b, qt, h, 0:keys]
                        last = nc.scalar.activation(pr, pr, ACT.Exp, bias=nmax[:, n, h:h + 1], scale=SCALE,
                                                    accum_out=rowsum[:, n, h:h + 1])
                    last.then_inc(exp_ready, 1)

            def split_hg():
                nc.scalar.copy(p_t[:, 0, 0, :], hg).then_inc(hg_hi, 1)

            def load_x(sec):
                act.wait_ge(out_stored, sec.c * (16 * KT) + 16)
                for kt in range(KT):
                    act.dma_start(acc[:, kt, :], x_in[bass.ds(sec.c, 1), :, kt, :].rearrange("c p t -> p (c t)")
                                  ).then_inc(x_loaded[kt], 16)

            def cond(sec):
                load_x(sec)
                act.wait_ge(mm_ready, sec.value("mm_ready", 0))
                for kt in range(KT):
                    act.wait_ge(x_loaded[kt], sec.c * 16 + 16)
                    nc.scalar.copy(xy(0, kt), acc[:, kt, :]).then_inc(x_hi, 1)
                act.wait_ge(shift_ready, sec.value("shift_ready", 1))
                nc.scalar.activation(expd, shifted, ACT.Exp).then_inc(gate_exp, 1)
                split_hi(sec, 1, lora_b[:, 0, :])
                act.wait_ge(s_read, sec.value("s_read", 2))
                split_hg()
                split_hi(sec, 5)
                for i in range(KT):
                    act.wait_ge(mm_ready, sec.value("mm_ready", i + 1))
                    nc.scalar.copy(hid[:, 0, i, :], mm[:, i % 2, :]).then_inc(mm_hi, 1)
                    if i == 0:
                        split_hi(sec, 6)
                    split_hi(sec, 7 + i)

            def first_group(sec):
                rope_swap(sec, 8, 0)
                split_hi(sec, 15)
                write_rope_hi(sec, 0, 0)
                act.wait_ge(mm_ready, sec.value("mm_ready", 10))
                split_hi(sec, 16)
                rope_swap(sec, 10, 1)
                split_hi(sec, 17)
                v_hi(sec, 2, 0)
                rope_swap(sec, 11, 2)
                write_rope_hi(sec, 0, 1)
                split_hi(sec, 18)
                rope_swap(sec, 12, 3)
                write_rope_hi(sec, 1, 2)
                split_hi(sec, 19)
                rope_swap(sec, 13, 4)
                write_rope_hi(sec, 0, 3)
                split_hi(sec, 20)
                write_rope_hi(sec, 1, 4)

            def body(sec):
                softmax_exp(sec)
                rope_swap(sec, 0, 0)
                probs_hi(sec, 0)
                split_hi(sec, 5)
                probs_hi(sec, 1)
                write_rope_hi(sec, 0, 0)
                write_o_hi(sec, 0)
                probs_hi(sec, 2)
                act.wait_ge(mm_ready, sec.value("mm_ready", 2))
                split_hi(sec, 6)
                probs_hi(sec, 3)
                write_o_hi(sec, 1)
                rope_swap(sec, 2, 1)
                probs_hi(sec, 4)
                split_hi(sec, 7)
                write_o_hi(sec, 2)
                probs_hi(sec, 5)
                rope_swap(sec, 3, 2)
                write_rope_hi(sec, 0, 1)
                write_o_hi(sec, 3)
                split_hi(sec, 8)
                v_hi(sec, 6, 0)
                rope_swap(sec, 4, 3)
                write_rope_hi(sec, 1, 2)
                split_hi(sec, 9)
                rope_swap(sec, 5, 4)
                write_rope_hi(sec, 0, 3)
                split_hi(sec, 10)
                write_rope_hi(sec, 1, 4)
                for m in range(4):
                    act.wait_ge(mm_ready, sec.value("mm_ready", 6 + 2 * m + 2))
                    split_hi(sec, 11 + m)

            def last_group(sec):
                softmax_exp(sec)
                probs_hi(sec, 0)
                probs_hi(sec, 1)
                write_o_hi(sec, 0)
                probs_hi(sec, 2)
                probs_hi(sec, 3)
                write_o_hi(sec, 1)
                probs_hi(sec, 4)
                write_o_hi(sec, 2)
                probs_hi(sec, 5)
                write_o_hi(sec, 3)
                for i in range(KT):
                    act.wait_ge(mm_read, sec.value("mm_read", i + 1))
                    nc.scalar.copy(hid[:, 0, i, :], acc[:, i, :]).then_inc(x1_hi, 1)
                    if i % 2 == 1 and i >= 3:
                        split_hi(sec, 5 + i // 2)

            def cond2(sec):
                split_hi(sec, 5, lora_b[:, 0, :])
                act.wait_ge(o_read, sec.value("o_read", 5))
                split_hg()
                split_hi(sec, 9)
                for i in range(KT):
                    act.wait_ge(mm_ready, sec.value("mm_ready", 8 + i + 1))
                    nc.scalar.activation(xy(0, i), mm[:, i % 2, :], ACT.Identity, bias=bia[:, B_2 + i:B_2 + i + 1]
                                         ).then_inc(mm_hi, 1)
                    if i == 0:
                        split_hi(sec, 10)
                    if i != 4:
                        split_hi(sec, 11 + i)

            def ffn(sec):
                act.wait_ge(shift_ready, sec.value("shift_ready", 1))
                nc.scalar.activation(expd, shifted, ACT.Exp)
                nc.scalar.activation(thr_e, lg.rearrange("p (t e) -> p t e", t=TT)[:, :, E], ACT.Exp,
                                     bias=neg_bthr[:], scale=-1.0).then_inc(gate_exp, 1)
                split_hi(sec, 15, lora_b[:, 0, :])
                act.wait_ge(o_read, sec.value("o_read", 6))
                split_hg()
                split_hi(sec, 19)
                for i in range(KT):
                    act.wait_ge(mm_ready, sec.value("mm_ready", 16 + i + 1))
                    if i == 0:
                        split_hi(sec, 20)
                    if i != 4:
                        split_hi(sec, 21 + i)
                    act.wait_ge(mm_read, sec.value("mm_read", 16 + i + 1))
                    act.dma_start(out[bass.ds(sec.c, 1), :, i, :].rearrange("c p t -> p (c t)"), acc[:, i, :]
                                  ).then_inc(out_stored, 16)

            act.sem_inc(out_stored, 16)
            act.wait_ge(const_loaded, 16 * N_CONST)
            nc.scalar.copy(gw[:, :, 0, :], gw_raw[:]).then_inc(gw_hi, 1)
            start = Section("pre", 0)
            for t in (0, 2, 3, 4):
                split_hi(start, t)
            with act.Fori(0, CHUNKS) as c:
                pre = Section("pre", c)
                cond(pre)
                first_group(pre)
                with act.Fori(0, BODIES) as g:
                    body(Section("body", c, g))
                post = Section("post", c)
                last_group(post)
                cond2(post)
                ffn(post)
            act.wait_ge(out_stored, 16 + CHUNKS * 16 * KT)

        @block.gpsimd
        def _(pool):
            def normalise(sec):
                for n in range(CS * QT):
                    b, qt = n // QT, n % QT
                    pool.wait_ge(rsum_ready, sec.value("rsum_ready", n + 1))
                    pool.sem_inc(passed, 1)
                    for h in range(HG):
                        pr = probs[:, b, qt, h, 0:(qt + 1) * P]
                        last = nc.gpsimd.tensor_scalar(pr, pr, rsum[:, n, h:h + 1], 1.0, ALU.mult, ALU.mult)
                    last.then_inc(p_ready, 1)

            def write_rope_sum(sec, k):
                s = 0 if k in (0, 1, 3) else 1
                pool.wait_ge(t2_ready, sec.value("t2_ready", k + 1))
                nc.gpsimd.tensor_tensor(turn[:, s, :], turn[:, s, :], swap[:, s, :], ALU.add
                                        ).then_inc(rope_sum, 1)

            with pool.Fori(0, CHUNKS) as c:
                pre = Section("pre", c)
                for k in range(5):
                    write_rope_sum(pre, k)
                with pool.Fori(0, BODIES) as g:
                    sec = Section("body", c, g)
                    normalise(sec)
                    for k in range(5):
                        write_rope_sum(sec, k)
                post = Section("post", c)
                normalise(post)

        @block.vector
        def _(dve):
            def split_lo(sec, tile, dst=None):
                s = sec.slot(tile)
                dve.wait_ge(w_hi[s], sec.round(tile))
                hi = w_sb[:, s, 0, :] if dst is None else lora_b[:, 0, :]
                lo = w_sb[:, s, 1, :] if dst is None else lora_b[:, 1, :]
                nc.vector.tensor_tensor(lo, w_raw_sb[:, s, :], f(hi), ALU.subtract).then_inc(w_lo[s], 1)

            def rope_products(sec, n, k):
                s = n % 2
                dve.wait_ge(xs_ready, sec.value("xs_ready", k + 1))
                nc.vector.tensor_tensor(by_sample(turn[:, s, :]), by_sample(mm[:, s, :]), cos, ALU.mult
                                        ).then_inc(mm_read, 1)
                nc.vector.tensor_tensor(by_sample(swap[:, s, :]), by_sample(swap[:, s, :]), sin, ALU.mult
                                        ).then_inc(t2_ready, 1)

            def write_rope_lo(sec, s, k):
                dve.wait_ge(rope_hi, sec.value("rope_hi", k + 1))
                hi, lo = (k_t[:, 0, :], k_t[:, 1, :]) if k == 0 else (q_t(0, k - 1), q_t(1, k - 1))
                nc.vector.tensor_tensor(lo, turn[:, s, :], f(hi), ALU.subtract).then_inc(rope_lo, 1)

            def probs_lo(sec, i):
                dve.wait_ge(ptb_hi, sec.value("ptb_hi", i + 1))
                nc.vector.tensor_tensor(p_t[:, i % 2, 1, :], ptb[:], f(p_t[:, i % 2, 0, :]), ALU.subtract
                                        ).then_inc(ptb_read, 1)

            def v_copy(sec, n):
                dve.wait_ge(mm_ready, sec.value("mm_ready", n + 1))
                nc.vector.tensor_copy(v_raw[:], mm[:, n % 2, :]).then_inc(mm_read, 1)

            def v_lo(sec, k):
                dve.wait_ge(ptb_hi, sec.value("ptb_hi", k))
                four = ptb[:].rearrange("p (t d) -> p t d", t=TT)
                nc.vector.tensor_tensor(v_tok[:, 1, :, :], four, f(v_tok[:, 0, :, :]), ALU.subtract
                                        ).then_inc(ptb_read, 1)

            def o_lo(sec, n):
                b, qt = n // QT, n % QT
                t0 = b * SEQ + qt * P
                dve.wait_ge(o_hi, sec.value("o_hi", n + 1))
                nc.vector.tensor_tensor(wide[:, 3, :, t0:t0 + P], ob[:, qt, :].rearrange("p (h t) -> p h t", h=HG),
                                        f(wide[:, 2, :, t0:t0 + P]), ALU.subtract).then_inc(o_read, 1)

            def softmax_max(sec, n):
                b, qt = n // QT, n % QT
                keys = (qt + 1) * P
                mask = cst[:, C_MASK + SEQ - keys:C_MASK + SEQ]
                for pair in range(2):
                    t = 2 * n + pair
                    dve.wait_ge(s_ready, sec.value("s_ready", t + 1))
                    dve.sem_inc(passed, 1)
                    for j in range(2):
                        h = 2 * pair + j
                        last = nc.vector.tensor_tensor_reduce(
                            out=probs[:, b, qt, h, 0:keys], in0=sc[:, t % 2, j * SEQ:j * SEQ + keys], in1=mask,
                            scale=1.0, scalar=-3e38, op0=ALU.add, op1=ALU.max, accum_out=rmax[:, n, h:h + 1])
                    last.then_inc(s_read, 1)
                dve.wait_ge(s_read, sec.value("s_read", 2 * n + 2))
                nc.vector.tensor_scalar(nmax[:, n, :], rmax[:, n, :], -SCALE, None, ALU.mult
                                        ).then_inc(nmax_ready, 1)

            def softmax_rsum(sec, n):
                dve.wait_ge(exp_ready, sec.value("exp_ready", n + 1))
                nc.vector.reciprocal(rsum[:, n, :], rowsum[:, n, :]).then_inc(rsum_ready, 1)

            def softmax(sec):
                softmax_max(sec, 0)
                softmax_max(sec, 1)
                softmax_rsum(sec, 0)
                softmax_max(sec, 2)
                softmax_rsum(sec, 1)
                softmax_max(sec, 3)
                softmax_rsum(sec, 2)
                softmax_rsum(sec, 3)

            def read_logits(sec, rows, ordinal):
                dve.wait_ge(s_ready, sec.value("s_ready", ordinal + 1))
                nc.vector.tensor_copy(logits_t[0:rows, :], sc[0:rows, 0, :]).then_inc(s_read, 1)

            def read_gates(sec, ordinal):
                dve.wait_ge(ptb_ready, sec.value("ptb_ready", ordinal + 1))
                nc.vector.tensor_copy(gates_t, ptb[:]).then_inc(ptb_read, 1)
                dve.wait_ge(ptb_read, sec.value("ptb_read", ordinal + 1))

            def split_hg(sec, k):
                dve.wait_ge(hg_hi, sec.value("hg_hi", k))
                nc.vector.tensor_tensor(p_t[:, 0, 1, :], hg, f(p_t[:, 0, 0, :]), ALU.subtract
                                        ).then_inc(hg_lo, 1)

            class Steps:

                def __init__(self, sec):
                    self.sec, self.n = sec, 0

                def __call__(self, ins):
                    self.n += 1
                    ins.then_inc(gate_step, 1)
                    dve.wait_ge(gate_step, self.sec.value("gate_step", self.n))

            def over_e(ap):
                return ap.rearrange("p (t e) -> p t e", t=TT)

            def per_token(ap):
                return ap[:, :, None].to_broadcast([P, TT, E])

            def spread_gates(step):
                step(nc.vector.scalar_tensor_tensor(out=over_e(gate), in0=over_e(wts), scalar=LORA_SCALE,
                                                    in1=per_token(winv), op0=ALU.mult, op1=ALU.mult))
                nc.vector.tensor_copy(gates_rep.rearrange("p (n r) -> p n r", r=R),
                                      gate[:, :, None].to_broadcast([P, TT * E, R])).then_inc(gates_ready, 1)

            def cond_gates(sec):
                step = Steps(sec)
                lge = over_e(lg[:, 0:TT * E])
                dve.wait_ge(ptb_ready, sec.value("ptb_ready", 1))
                samples = lang_bias[:, bass.ds(sec.c * CS, CS), :]
                nc.vector.tensor_tensor(
                    lg[:, 0:TT * E].rearrange("p (s t e) -> p s t e", s=CS, t=QT),
                    ptb[:, 0:TT * E].rearrange("p (s t e) -> p s t e", s=CS, t=QT),
                    samples[:, :, None, :].to_broadcast([P, CS, QT, E]), ALU.add).then_inc(ptb_read, 1)
                dve.wait_ge(ptb_read, sec.value("ptb_read", 1))
                step(nc.vector.reduce_max(top, lge, AX))
                nc.vector.tensor_tensor(over_e(shifted), lge, per_token(top), ALU.subtract).then_inc(shift_ready, 1)
                pair = lambda ap: ap.rearrange("p (t e o) -> p t e o", t=TT, e=E)
                other = lge[:, :, None, :].to_broadcast([P, TT, E, E])
                own = lge[:, :, :, None].to_broadcast([P, TT, E, E])
                lower = cst[:, None, C_TRI:C_TRI + E * E].to_broadcast([P, TT, E * E])
                step(nc.vector.tensor_tensor(pair(beats), other, own, ALU.is_gt))
                step(nc.vector.tensor_tensor(pair(ties), other, own, ALU.is_equal))
                flat = lambda ap: ap.rearrange("p (t n) -> p t n", t=TT)
                step(nc.vector.tensor_tensor(flat(ties), flat(ties), lower, ALU.mult))
                step(nc.vector.tensor_tensor(beats, beats, ties, ALU.add))
                step(nc.vector.reduce_sum(rank, beats.rearrange("p (n o) -> p n o", o=E), AX))
                step(nc.vector.tensor_scalar(chosen, rank, 1.5, None, ALU.is_lt))
                dve.wait_ge(gate_exp, sec.value("gate_exp", 1))
                step(nc.vector.tensor_tensor(wts, expd, chosen, ALU.mult))
                step(nc.vector.reduce_sum(wsum, over_e(wts), AX))
                step(nc.vector.reciprocal(winv, wsum))
                spread_gates(step)
                assert step.n == COUNTS["gate_step"][0]

            def ffn_gates(sec):
                step = Steps(sec)
                lg9 = lg.rearrange("p (t e) -> p t e", t=TT)
                dve.wait_ge(ptb_ready, sec.value("ptb_ready", 7))
                nc.vector.tensor_copy(lg, ptb[:, 0:TT * (E + 1)]).then_inc(ptb_read, 1)
                dve.wait_ge(ptb_read, sec.value("ptb_read", 7))
                step(nc.vector.reduce_max(top, lg9[:, :, 0:E], AX))
                nc.vector.tensor_tensor(over_e(shifted), lg9[:, :, 0:E], per_token(top), ALU.subtract
                                        ).then_inc(shift_ready, 1)
                dve.wait_ge(gate_exp, sec.value("gate_exp", 1))
                step(nc.vector.reduce_sum(wsum, over_e(expd), AX))
                step(nc.vector.reciprocal(winv, wsum))
                step(nc.vector.tensor_tensor(over_e(rank), over_e(expd), per_token(winv), ALU.mult))
                step(nc.vector.tensor_scalar(thr_1, thr_e, 1.0, None, ALU.add))
                step(nc.vector.reciprocal(thr_r, thr_1))
                step(nc.vector.tensor_scalar(thr, thr_r, MAX_THRESHOLD, None, ALU.mult))
                step(nc.vector.tensor_tensor(over_e(chosen), over_e(rank), per_token(thr), ALU.subtract))
                step(nc.vector.tensor_scalar(wts, chosen, 0.0, None, ALU.max))
                step(nc.vector.reduce_sum(wsum, over_e(wts), AX))
                step(nc.vector.tensor_scalar(is_zero, wsum, 0.0, None, ALU.is_equal))
                step(nc.vector.tensor_tensor(wsum1, wsum, is_zero, ALU.add))
                step(nc.vector.reciprocal(winv, wsum1))
                spread_gates(step)
                assert step.n == COUNTS["gate_step"][2]

            def cond(sec):
                for kt in range(KT):
                    dve.wait_ge(x_hi, sec.value("x_hi", kt + 1))
                    nc.vector.tensor_tensor(xy(1, kt), acc[:, kt, :], f(xy(0, kt)), ALU.subtract
                                            ).then_inc(x_lo, 1)
                read_logits(sec, E, 0)
                cond_gates(sec)
                split_lo(sec, 1, lora_b)
                read_gates(sec, 1)
                dve.wait_ge(s_ready, sec.value("s_ready", 2))
                nc.vector.tensor_tensor(hg, sc[:, 1, :], gates_t, ALU.mult).then_inc(s_read, 1)
                split_hg(sec, 1)
                split_lo(sec, 5)
                for i in range(KT):
                    dve.wait_ge(mm_hi, sec.value("mm_hi", i + 1))
                    nc.vector.tensor_tensor(hid[:, 1, i, :], mm[:, i % 2, :], f(hid[:, 0, i, :]), ALU.subtract
                                            ).then_inc(mm_read, 1)
                    if i == 0:
                        split_lo(sec, 6)
                    split_lo(sec, 7 + i)

            def first_group(sec):
                rope_products(sec, 8, 0)
                split_lo(sec, 15)
                write_rope_lo(sec, 0, 0)
                v_copy(sec, 9)
                split_lo(sec, 16)
                rope_products(sec, 10, 1)
                split_lo(sec, 17)
                v_lo(sec, 1)
                rope_products(sec, 11, 2)
                write_rope_lo(sec, 0, 1)
                split_lo(sec, 18)
                rope_products(sec, 12, 3)
                write_rope_lo(sec, 1, 2)
                split_lo(sec, 19)
                rope_products(sec, 13, 4)
                write_rope_lo(sec, 0, 3)
                split_lo(sec, 20)
                write_rope_lo(sec, 1, 4)

            def body(sec):
                softmax(sec)
                rope_products(sec, 0, 0)
                probs_lo(sec, 0)
                split_lo(sec, 5)
                probs_lo(sec, 1)
                write_rope_lo(sec, 0, 0)
                o_lo(sec, 0)
                probs_lo(sec, 2)
                v_copy(sec, 1)
                split_lo(sec, 6)
                probs_lo(sec, 3)
                o_lo(sec, 1)
                rope_products(sec, 2, 1)
                probs_lo(sec, 4)
                split_lo(sec, 7)
                o_lo(sec, 2)
                probs_lo(sec, 5)
                rope_products(sec, 3, 2)
                write_rope_lo(sec, 0, 1)
                o_lo(sec, 3)
                split_lo(sec, 8)
                v_lo(sec, 7)
                rope_products(sec, 4, 3)
                write_rope_lo(sec, 1, 2)
                split_lo(sec, 9)
                rope_products(sec, 5, 4)
                write_rope_lo(sec, 0, 3)
                split_lo(sec, 10)
                write_rope_lo(sec, 1, 4)
                for i in range(KT):
                    add_projection(sec, i, 6)
                    if i % 2 == 1:
                        split_lo(sec, 11 + i // 2)

            def add_projection(sec, i, first_out):
                n = first_out + i
                dve.wait_ge(mm_ready, sec.value("mm_ready", n + 1))
                nc.vector.tensor_tensor(acc[:, i, :], mm[:, n % 2, :], acc[:, i, :], ALU.add
                                        ).then_inc(mm_read, 1)

            def last_group(sec):
                softmax(sec)
                probs_lo(sec, 0)
                probs_lo(sec, 1)
                o_lo(sec, 0)
                probs_lo(sec, 2)
                probs_lo(sec, 3)
                o_lo(sec, 1)
                probs_lo(sec, 4)
                o_lo(sec, 2)
                probs_lo(sec, 5)
                o_lo(sec, 3)
                for i in range(KT):
                    add_projection(sec, i, 0)
                    dve.wait_ge(x1_hi, sec.value("x1_hi", i + 1))
                    nc.vector.tensor_tensor(hid[:, 1, i, :], acc[:, i, :], f(hid[:, 0, i, :]), ALU.subtract
                                            ).then_inc(x1_lo, 1)
                    if i % 2 == 1 and i >= 3:
                        split_lo(sec, 5 + i // 2)

            def cond2(sec):
                split_lo(sec, 5, lora_b)
                dve.wait_ge(o_ready, sec.value("o_ready", 5))
                for s in range(CS):
                    own = cst[:, bass.ds(sec.c * CS + (C_OWN + s), 1)]
                    last = nc.vector.tensor_scalar(hg[:, s * SEQ:(s + 1) * SEQ], ob[:, 0, s * SEQ:(s + 1) * SEQ],
                                                   own, None, ALU.mult)
                last.then_inc(o_read, 1)
                split_hg(sec, 1)
                split_lo(sec, 9)
                for i in range(KT):
                    dve.wait_ge(mm_hi, sec.value("mm_hi", i + 1))
                    nc.vector.scalar_tensor_tensor(out=xy(1, i), in0=mm[:, i % 2, :],
                                                   scalar=bia[:, B_2 + i:B_2 + i + 1], in1=f(xy(0, i)),
                                                   op0=ALU.add, op1=ALU.subtract).then_inc(mm_read, 1)
                    if i == 0:
                        split_lo(sec, 10)
                    if i != 4:
                        split_lo(sec, 11 + i)

            def ffn(sec):
                read_logits(sec, E + 1, 8)
                ffn_gates(sec)
                split_lo(sec, 15, lora_b)
                read_gates(sec, 7)
                dve.wait_ge(o_ready, sec.value("o_ready", 6))
                nc.vector.tensor_tensor(hg, ob[:, 1, :], gates_t, ALU.mult).then_inc(o_read, 1)
                split_hg(sec, 2)
                split_lo(sec, 19)
                for i in range(KT):
                    dve.wait_ge(mm_ready, sec.value("mm_ready", 16 + i + 1))
                    nc.vector.scalar_tensor_tensor(out=acc[:, i, :], in0=mm[:, i % 2, :],
                                                   scalar=bia[:, B_B + i:B_B + i + 1], in1=acc[:, i, :],
                                                   op0=ALU.add, op1=ALU.add).then_inc(mm_read, 1)
                    if i == 0:
                        split_lo(sec, 20)
                    if i != 4:
                        split_lo(sec, 21 + i)

            done = [0]

            def link(ins):
                done[0] += 1
                ins.then_inc(setup, 1)
                dve.wait_ge(setup, done[0])

            dve.wait_ge(const_loaded, 16 * N_CONST)
            link(nc.vector.tensor_copy(ids_f[:], ids_raw[:]))
            link(nc.vector.tensor_scalar(slot_neg[:], ids_f[:, 1, :], 0.0, float(SLOTS), ALU.is_lt, ALU.mult))
            link(nc.vector.tensor_tensor(ids_f[:, 1, :], ids_f[:, 1, :], slot_neg[:], ALU.add))
            link(nc.vector.tensor_scalar(slot_neg[:], ids_f[:, 1, :], 0.0, float(SLOTS - 1), ALU.max, ALU.min))
            nc.vector.tensor_copy(slot_ids[:], slot_neg[:]).then_inc(slots_ready, 1)
            iota = cst[:, None, C_IOTA:C_IOTA + E].to_broadcast([P, SAMPLES, E])
            lang = ids_f[:, 0, :, None].to_broadcast([P, SAMPLES, E])
            link(nc.vector.tensor_tensor(lang_bias[:], iota, lang, ALU.is_equal))
            link(nc.vector.tensor_scalar(lang_bias[:], lang_bias[:], LANG_BIAS, None, ALU.mult))
            link(nc.vector.tensor_scalar(neg_bthr[:], bia[:, B_THR:B_THR + 1], -1.0, None, ALU.mult))
            dve.wait_ge(gw_hi, 1)
            nc.vector.tensor_tensor(gw[:, :, 1, :], gw_raw[:], f(gw[:, :, 0, :]), ALU.subtract).then_inc(gw_lo, 1)
            start = Section("pre", 0)
            for t in (0, 2, 3, 4):
                split_lo(start, t)
            with dve.Fori(0, CHUNKS) as c:
                pre = Section("pre", c)
                cond(pre)
                first_group(pre)
                with dve.Fori(0, BODIES) as g:
                    body(Section("body", c, g))
                post = Section("post", c)
                last_group(post)
                cond2(post)
                ffn(post)


def shape_constants():
    f32 = np.float32
    inv_freq = (f32(1.0) / f32(10000.0) ** (np.arange(0, HD, 2, dtype=f32) / f32(HD))).astype(f32)
    freqs = np.outer(np.arange(SEQ, dtype=f32), inv_freq).astype(f32).T
    c = np.zeros((P, C_COLS), f32)
    c[:, C_COS:C_COS + SEQ] = np.concatenate([np.cos(freqs), np.cos(freqs)])
    c[:, C_SIN:C_SIN + SEQ] = np.concatenate([-np.sin(freqs), np.sin(freqs)])
    q, k = np.arange(P)[:, None], np.arange(P)[None, :]
    c[:, C_MASK + P:C_MASK + 2 * P] = np.where(k > q, f32(MASKED), f32(0))
    c[:, C_ID:C_ID + P] = np.eye(P, dtype=f32)
    c[:, C_TRI:C_TRI + E * E] = (np.arange(E)[None, :] < np.arange(E)[:, None]).astype(f32).reshape(1, -1)
    c[:, C_IOTA:C_IOTA + E] = np.arange(E, dtype=f32)
    c[:, C_OWN:C_OWN + SAMPLES] = np.where(np.arange(P)[:, None] // R == np.arange(SAMPLES), f32(LORA_SCALE), f32(0))
    return c


def weight_tiles(i):
    def rows(w):
        return w.reshape(-1, P, KT, P).transpose(0, 3, 2, 1).reshape(-1, P, D)

    def lora_a(a):
        return rows(a.reshape(E * R, D))

    def lora_b(b):
        return b.transpose(0, 2, 1).reshape(1, E * R, D)

    wqkv = rows(i["L0_attn_Wqkv"])
    order = [[HEADS + g, HEADS + KV + g] + [HG * g + h for h in range(HG)] for g in range(KV)]
    wo = i["L0_attn_Wo"].reshape(KT // 2, 2, P, KV, HG, HD).transpose(3, 0, 5, 1, 4, 2).reshape(KV, KT // 2, P, D)
    parts = [lora_a(i["L0_cond_A"]), lora_b(i["L0_cond_B"]), rows(i["L0_cond_W"]), wqkv[order[0]]]
    for g in range(BODIES):
        parts += [wqkv[order[g + 1]], wo[g]]
    parts += [wo[KV - 1], rows(i["L0_cond2_W"]), lora_a(i["L0_ffn_A_w"]), lora_b(i["L0_ffn_B_w"]),
              rows(i["L0_ffn_W_base"])]
    return np.ascontiguousarray(np.concatenate(parts))


def kernel(**inputs):
    import concourse.bacc as bacc
    from concourse.bass_utils import run_bass_kernel_spmd

    i = {k: np.asarray(v) for k, v in inputs.items()}
    f32 = np.float32
    x = i["x"].reshape(CHUNKS, CHUNK, KT, P).transpose(0, 3, 2, 1)
    gate_w = np.zeros((P, 2, WG_COLS), f32)
    wr = i["L0_cond_Wr"].reshape(E, KT, P)
    wg = np.concatenate([i["L0_ffn_W_gate"], i["L0_ffn_W_thr"][None]]).reshape(E + 1, KT, P)
    for kt in range(KT):
        gate_w[:, 0, kt * WG_STEP:kt * WG_STEP + E] = wr[:, kt].T
        gate_w[:, 1, kt * WG_STEP:kt * WG_STEP + E + 1] = wg[:, kt].T
    biases = np.concatenate([i["L0_cond2_b"].reshape(KT, P).T, i["L0_ffn_b_base"].reshape(KT, P).T,
                             np.broadcast_to(i["L0_ffn_b_thr"], (P, 1))], axis=1)
    ids = np.broadcast_to(np.stack([i["itok_B_0_7"], i["itok_B_0_23"]]), (P, 2, SAMPLES))
    arrays = {
        "x": x,
        "stream": weight_tiles(i),
        "adapters_a": i["L0_cond2_lora_As"].reshape(SLOTS, KT, P, R).transpose(0, 2, 1, 3),
        "adapters_b": i["L0_cond2_lora_Bs"],
        "gate_w": gate_w,
        "consts": shape_constants(),
        "biases": biases,
        "ids": ids,
    }
    arrays = {k: np.ascontiguousarray(v) for k, v in arrays.items()}
    nc = bacc.Bacc("TRN2", target_bir_lowering=False, num_devices=1)
    args = [nc.dram_tensor(k, a.shape, mybir.dt.from_np(a.dtype), kind="ExternalInput").ap()
            for k, a in arrays.items()]
    out = nc.dram_tensor("out", (CHUNKS, P, KT, CHUNK), F32, kind="ExternalOutput").ap()
    build(nc, *args, out)
    got = run_bass_kernel_spmd(nc, [arrays], core_ids=[0]).results[0]["out"]
    return got.transpose(0, 3, 2, 1).reshape(SAMPLES, SEQ, D)
```

```python
from contextlib import ExitStack

import numpy as np
import concourse.bass as bass
from concourse import mybir

F32 = mybir.dt.float32
F32R = mybir.dt.float32r
I32 = mybir.dt.int32
ALU = mybir.AluOpType
ACT = mybir.ActivationFunctionType
AX = mybir.AxisListType.X

P = 128
SAMPLES, SEQ, D = 8, 256, 1024
KT = D // P
CHUNK = 512
CHUNKS = SAMPLES * SEQ // CHUNK
CS = CHUNK // SEQ
TT = CHUNK // P
HEADS, KV, HD = 32, 8, 128
HG = HEADS // KV
QT = SEQ // P
E, R = 8, 16
SLOTS = 32
SCALE = float(1.0 / np.sqrt(np.float32(HD)))
MASKED = -1e30
LANG_BIAS = 5.0
LORA_SCALE = 2.0
MAX_THRESHOLD = 0.125

RING = 5
TILES = {"pre": 16, "body": 10, "post": 24}
BODIES = KV - 1
TILES_CHUNK = TILES["pre"] + BODIES * TILES["body"] + TILES["post"]
GATHER_AT = 90
assert TILES_CHUNK % RING == 0 and TILES["body"] % RING == 0 and GATHER_AT % RING == 0

COUNTS = {
    "mm_ready":   (14, 14, 32, 1),
    "mm_hi":      (8, 0, 8, 0),
    "mm_read":    (14, 14, 32, 2),
    "s_ready":    (10, 8, 1, 0),
    "s_read":     (10, 8, 1, 1),
    "ptb_ready":  (3, 7, 8, 0),
    "ptb_hi":     (1, 7, 6, 0),
    "ptb_read":   (3, 7, 8, 1),
    "o_ready":    (0, 4, 6, 0),
    "o_hi":       (0, 4, 4, 0),
    "o_read":     (0, 4, 6, 2),
    "nmax_ready": (4, 4, 0, 0),
    "exp_ready":  (4, 4, 0, 0),
    "rsum_ready": (4, 4, 0, 0),
    "p_ready":    (4, 4, 0, 0),
    "xs_ready":   (5, 5, 0, 0),
    "t2_ready":   (5, 5, 0, 0),
    "rope_sum":   (5, 5, 0, 0),
    "rope_hi":    (5, 5, 0, 0),
    "rope_lo":    (5, 5, 0, 1),
    "x_hi":       (8, 0, 0, 0),
    "x_lo":       (8, 0, 0, 0),
    "x1_hi":      (0, 0, 8, 0),
    "x1_lo":      (0, 0, 8, 0),
    "shift_ready": (1, 0, 1, 0),
    "gate_exp":   (1, 0, 1, 0),
    "gate_step":  (11, 0, 14, 0),
    "gates_ready": (1, 0, 1, 0),
    "hg_hi":      (1, 0, 2, 0),
    "hg_lo":      (1, 0, 2, 0),
}

C_COS, C_SIN, C_MASK, C_ID, C_TRI, C_IOTA, C_OWN = 0, 256, 512, 768, 896, 960, 968
C_COLS = C_OWN + SAMPLES
B_2, B_B, B_THR = 0, KT, 2 * KT
WG_STEP = 16
WG_COLS = (KT - 1) * WG_STEP + P


class Section:

    def __init__(self, kind, c, g=0):
        self.kind, self.c, self.g = kind, c, g

    def count(self, pre, body, post, k):
        per_chunk = pre + BODIES * body + post
        if self.kind == "pre":
            return self.c * per_chunk + k
        if self.kind == "body":
            return self.c * per_chunk + self.g * body + (pre + k)
        return self.c * per_chunk + (pre + BODIES * body + k)

    def value(self, name, k):
        pre, body, post, at_start = COUNTS[name]
        return self.count(pre, body, post, k + at_start)

    def slot(self, tile):
        before = {"pre": 0, "body": TILES["pre"], "post": TILES["pre"] + BODIES * TILES["body"]}[self.kind]
        return (before + tile) % RING

    def round(self, tile):
        before = {"pre": 0, "body": TILES["pre"], "post": TILES["pre"] + BODIES * TILES["body"]}[self.kind]
        turns = (before + tile) // RING + 1
        per_chunk, per_body = TILES_CHUNK // RING, TILES["body"] // RING
        if self.kind == "body":
            return self.c * per_chunk + self.g * per_body + turns
        return self.c * per_chunk + turns


def build(nc, x_in, stream, adapters_a, adapters_b, gate_w, consts, biases, ids, out):
    ctx = ExitStack()
    with ctx:
        def sb(name, shape, dt=F32):
            return ctx.enter_context(nc.sbuf_tensor(name, shape, dt))

        def psum(name, shape):
            return ctx.enter_context(nc.psum_tensor(name, shape, F32))

        gathered_a = nc.dram_tensor("gathered_a", (P, KT, SAMPLES, R), F32, kind="Internal").ap()
        gathered_b = nc.dram_tensor("gathered_b", (SAMPLES, R, D), F32, kind="Internal").ap()

        hid = sb("hid", [P, 2, KT, CHUNK], F32R)
        wide = sb("wide", [P, 4, HG, CHUNK], F32R)
        acc = sb("acc", [P, KT, CHUNK])
        k_t = sb("k_t", [P, 2, CHUNK], F32R)
        v_tok = sb("v_tok", [P, 2, TT, HD], F32R)
        v_raw = sb("v_raw", [P, CHUNK])
        probs = sb("probs", [P, CS, QT, HG, SEQ])
        p_t = sb("p_t", [P, 2, 2, CHUNK], F32R)
        w_raw_sb = sb("w_raw_sb", [P, RING, D])
        w_sb = sb("w_sb", [P, RING, 2, D], F32R)
        lora_b = sb("lora_b", [P, 2, D], F32R)
        swap = sb("swap", [P, 2, CHUNK])
        turn = sb("turn", [P, 2, CHUNK])
        gw_raw = sb("gw_raw", [P, 2, WG_COLS])
        gw = sb("gw", [P, 2, 2, WG_COLS], F32R)
        cst = sb("cst", [P, C_COLS])
        bia = sb("bia", [P, 2 * KT + 1])
        neg_bthr = sb("neg_bthr", [P, 1])
        ids_raw = sb("ids_raw", [P, 2, SAMPLES], I32)
        ids_f = sb("ids_f", [P, 2, SAMPLES])
        slot_neg = sb("slot_neg", [P, SAMPLES])
        slot_ids = sb("slot_ids", [P, SAMPLES], I32)
        lang_bias = sb("lang_bias", [P, SAMPLES, E])
        rmax = sb("rmax", [P, 4, HG])
        nmax = sb("nmax", [P, 4, HG])
        rowsum = sb("rowsum", [P, 4, HG])
        rsum = sb("rsum", [P, 4, HG])

        scratch = probs[:].rearrange("p a b c d -> p (a b c d)")
        logits_t = scratch[:, 0:512]
        gates_t = scratch[:, 512:1024]
        hg = scratch[:, 1024:1536]
        gates_rep = scratch[:, 1536:2048]
        beats = scratch[:, 2048:2304]
        ties = scratch[:, 2304:2560]
        small = scratch[:, 2560:2560 + 16 * 40]
        lg = small[:, 0:36]
        shifted = small[:, 40:72]
        expd = small[:, 80:112]
        rank = small[:, 120:152]
        chosen = small[:, 160:192]
        wts = small[:, 200:232]
        gate = small[:, 240:272]
        top = small[:, 280:284]
        wsum = small[:, 320:324]
        winv = small[:, 360:364]
        thr_e = small[:, 400:404]
        thr_1 = small[:, 440:444]
        thr_r = small[:, 480:484]
        thr = small[:, 520:524]
        is_zero = small[:, 560:564]
        wsum1 = small[:, 600:604]

        mm = psum("mm", [P, 2, 512])
        sc = psum("sc", [P, 2, 512])
        ptb = psum("ptb", [P, 512])
        ptb1 = psum("ptb1", [P, 512])
        ob = psum("ob", [P, 2, 512])

        def semaphore(name):
            return ctx.enter_context(nc.semaphore(name))

        mm_ready = semaphore("mm_ready")
        mm_hi = semaphore("mm_hi")
        mm_read = semaphore("mm_read")
        s_ready = semaphore("s_ready")
        s_read = semaphore("s_read")
        ptb_ready = semaphore("ptb_ready")
        ptb_hi = semaphore("ptb_hi")
        ptb_read = semaphore("ptb_read")
        o_ready = semaphore("o_ready")
        o_hi = semaphore("o_hi")
        o_read = semaphore("o_read")
        nmax_ready = semaphore("nmax_ready")
        exp_ready = semaphore("exp_ready")
        rsum_ready = semaphore("rsum_ready")
        p_ready = semaphore("p_ready")
        xs_ready = semaphore("xs_ready")
        t2_ready = semaphore("t2_ready")
        rope_sum = semaphore("rope_sum")
        rope_hi = semaphore("rope_hi")
        rope_lo = semaphore("rope_lo")
        x_hi = semaphore("x_hi")
        x_lo = semaphore("x_lo")
        x1_hi = semaphore("x1_hi")
        x1_lo = semaphore("x1_lo")
        shift_ready = semaphore("shift_ready")
        gate_exp = semaphore("gate_exp")
        gate_step = semaphore("gate_step")
        gates_ready = semaphore("gates_ready")
        hg_hi = semaphore("hg_hi")
        hg_lo = semaphore("hg_lo")
        w_raw = [semaphore(f"w_raw{s}") for s in range(RING)]
        w_hi = [semaphore(f"w_hi{s}") for s in range(RING)]
        w_lo = [semaphore(f"w_lo{s}") for s in range(RING)]
        x_loaded = [semaphore(f"x_loaded{k}") for k in range(KT)]
        out_stored = semaphore("out_stored")
        const_loaded = semaphore("const_loaded")
        slots_ready = semaphore("slots_ready")
        adapters_ready = semaphore("adapters_ready")
        gw_hi = semaphore("gw_hi")
        gw_lo = semaphore("gw_lo")
        setup = semaphore("setup")
        passed = semaphore("passed")
        N_CONST = 4

        def f(ap):
            return ap.bitcast(F32)

        cos = cst[:, None, C_COS:C_COS + SEQ].to_broadcast([P, CS, SEQ])
        sin = cst[:, None, C_SIN:C_SIN + SEQ].to_broadcast([P, CS, SEQ])
        ident = cst[:, C_ID:C_ID + P]

        def by_sample(ap):
            return ap.rearrange("p (s t) -> p s t", s=CS)

        def xy(hl, kt):
            return wide[:, 2 * hl + kt // HG, kt % HG, :]

        def q_t(hl, h):
            return wide[:, hl, h, :]

        def o_t(hl, h):
            return wide[:, 2 + hl, h, :]

        block = ctx.enter_context(nc.Block())

        @block.sync
        def _(sp):
            sp.dma_start(ids_raw[:], ids).then_inc(const_loaded, 16)
            sp.dma_start(cst[:], consts).then_inc(const_loaded, 16)
            sp.dma_start(gw_raw[:], gate_w).then_inc(const_loaded, 16)
            sp.dma_start(bia[:], biases).then_inc(const_loaded, 16)
            for t in range(RING):
                sp.dma_start(w_raw_sb[:, t, :], stream[t]).then_inc(w_raw[t], 16)
            sp.wait_ge(slots_ready, 1)
            for b in range(SAMPLES):
                a = sp.value_load(slot_ids[0:1, b:b + 1], min_val=0, max_val=SLOTS - 1)
                sp.dma_start(gathered_a[:, :, b, :], adapters_a[bass.ds(a, 1)].rearrange("s p k r -> p (s k) r")
                             ).then_inc(adapters_ready, 16)
                sp.dma_start(gathered_b[b], adapters_b[bass.ds(a, 1)].rearrange("s r d -> (s r) d")
                             ).then_inc(adapters_ready, 16)
            sp.wait_ge(adapters_ready, 16 * 2 * SAMPLES)
            rounds = TILES_CHUNK // RING

            def load(c, i, s, src):
                sp.wait_ge(w_lo[s], c * rounds + i + 1)
                sp.dma_start(w_raw_sb[:, s, :], src).then_inc(w_raw[s], 16)

            def tile_of_stream(n):
                return stream[bass.ds(n, 1)].rearrange("n p d -> (n p) d")

            with sp.Fori(0, CHUNKS) as c:
                with sp.Fori(1, GATHER_AT // RING) as i:
                    for s in range(RING):
                        load(c, i, s, tile_of_stream(i * RING + s))
                load(c, GATHER_AT // RING, 0, gathered_a.rearrange("p k b r -> p (k b r)"))
                load(c, GATHER_AT // RING, 1, gathered_b.rearrange("b r d -> (b r) d"))
                for s in range(2, RING):
                    load(c, GATHER_AT // RING, s, stream[GATHER_AT + s - 2])
                with sp.Fori(GATHER_AT // RING + 1, rounds) as i:
                    for s in range(RING):
                        load(c, i, s, tile_of_stream(i * RING + (s - 2)))
                for s in range(RING):
                    load(c, rounds, s, stream[s])
            for s in range(RING):
                sp.wait_ge(w_raw[s], 16 * (CHUNKS * rounds + 1))

        @block.tensor
        def _(pe):
            for s in range(RING):
                pe.sem_inc(w_lo[s], 1)
            pe.sem_inc(mm_ready, COUNTS["mm_ready"][3])
            pe.sem_inc(mm_read, COUNTS["mm_read"][3])
            pe.sem_inc(s_read, COUNTS["s_read"][3])
            pe.sem_inc(ptb_read, COUNTS["ptb_read"][3])
            pe.sem_inc(o_read, COUNTS["o_read"][3])
            pe.sem_inc(rope_lo, COUNTS["rope_lo"][3])

            def product(bank, w_hi_ap, w_lo_ap, x_hi_ap, x_lo_ap, start, stop):
                nc.tensor.matmul(bank, w_hi_ap, x_hi_ap, start=start, stop=False, skip_group_check=True)
                nc.tensor.matmul(bank, w_hi_ap, x_lo_ap, start=False, stop=False, skip_group_check=True)
                return nc.tensor.matmul(bank, w_lo_ap, x_hi_ap, start=False, stop=stop, skip_group_check=True)

            def tile_ready(sec, tile):
                pe.wait_ge(w_lo[sec.slot(tile)], sec.round(tile) + 1)

            def column(slot, hl, n):
                return w_sb[:, slot, hl, n * P:(n + 1) * P]

            def linear(sec, bank, tile, src, kts=range(KT), stop=True, ready=None):
                slot = sec.slot(tile)
                if kts[0] == 0:
                    tile_ready(sec, tile)
                for kt in kts:
                    if ready:
                        ready(kt)
                    last = product(bank, column(slot, 0, kt), column(slot, 1, kt), src(0, kt), src(1, kt),
                                   kt == 0, stop and kt == KT - 1)
                return last

            def hid_src(hl, kt):
                return hid[:, hl, kt, :]

            def logits(sec, which, bank, src, ready):
                for kt in range(KT):
                    ready(kt)
                    cols = slice(kt * WG_STEP, kt * WG_STEP + P)
                    last = product(bank, gw[:, which, 0, cols], gw[:, which, 1, cols], src(0, kt), src(1, kt),
                                   kt == 0, kt == KT - 1)
                last.then_inc(s_ready, 1)

            def lora(sec, bank, i, n):
                product(bank, lora_b[:, 0, i * P:(i + 1) * P], lora_b[:, 1, i * P:(i + 1) * P],
                        p_t[:, 0, 0, :], p_t[:, 0, 1, :], False, True).then_inc(mm_ready, 1)

            def turn_logits(sec, rows, read_k, ordinal):
                pe.wait_ge(s_read, sec.value("s_read", read_k))
                pe.wait_ge(ptb_read, sec.value("ptb_read", ordinal))
                pe.sem_inc(passed, 1)
                for t in range(TT):
                    last = nc.tensor.transpose(ptb[:, t * rows:(t + 1) * rows], logits_t[0:rows, t * P:(t + 1) * P],
                                               cst[0:rows, C_ID:C_ID + rows])
                last.then_inc(ptb_ready, 1)

            def turn_gates(sec, ordinal):
                pe.wait_ge(gates_ready, sec.value("gates_ready", 1))
                pe.wait_ge(ptb_read, sec.value("ptb_read", ordinal))
                for t in range(TT):
                    last = nc.tensor.transpose(ptb[:, t * P:(t + 1) * P], gates_rep[:, t * P:(t + 1) * P], ident)
                last.then_inc(ptb_ready, 1)

            def scores(sec, n, first):
                b, qt, pair = n // 4, n // 2 % 2, n % 2
                if n == 0:
                    pe.wait_ge(rope_lo, sec.value("rope_lo", 5))
                pe.wait_ge(s_read, sec.value("s_read", first + n - 1))
                for j in range(2):
                    h = 2 * pair + j
                    q0 = b * SEQ + qt * P
                    last = product(sc[:, n % 2, j * SEQ:(j + 1) * SEQ],
                                   q_t(0, h)[:, q0:q0 + P], q_t(1, h)[:, q0:q0 + P],
                                   k_t[:, 0, b * SEQ:(b + 1) * SEQ], k_t[:, 1, b * SEQ:(b + 1) * SEQ], True, True)
                last.then_inc(s_ready, 1)

            BLOCKS = [(0, 0), (0, 1), (1, 1)]

            def turn_probs(sec, i, two_banks=False):
                b, (kt, qt) = i // 3, BLOCKS[i % 3]
                bank = ptb1 if two_banks and i % 2 else ptb
                pe.wait_ge(p_ready, sec.value("p_ready", b * QT + qt + 1 - CS * QT))
                pe.wait_ge(ptb_read, sec.value("ptb_read", max(i - 1, 0) if two_banks else i))
                for h in range(HG):
                    last = nc.tensor.transpose(bank[:, h * P:(h + 1) * P], probs[:, b, qt, h, kt * P:(kt + 1) * P],
                                               ident)
                last.then_inc(ptb_ready, 1)

            def attend(sec, i):
                b, (kt, qt) = i // 3, BLOCKS[i % 3]
                pe.wait_ge(ptb_read, sec.value("ptb_read", i + 1))
                if kt == 0:
                    pe.wait_ge(o_read, sec.value("o_read", b * QT + qt - 1))
                last = product(ob[:, qt, :], v_tok[:, 0, b * QT + kt, :], v_tok[:, 1, b * QT + kt, :],
                               p_t[:, i % 2, 0, :], p_t[:, i % 2, 1, :], kt == 0, kt == qt)
                if kt == qt:
                    last.then_inc(o_ready, 1)

            def turn_v(sec, out_n, ordinal):
                pe.wait_ge(mm_read, sec.value("mm_read", out_n + 1))
                pe.wait_ge(ptb_read, sec.value("ptb_read", ordinal))
                for t in range(TT):
                    last = nc.tensor.transpose(ptb[:, t * P:(t + 1) * P], v_raw[:, t * P:(t + 1) * P], ident)
                last.then_inc(ptb_ready, 1)

            def bank_free(sec, n):
                pe.wait_ge(mm_read, sec.value("mm_read", n - 1))

            def qkv(sec, i, half, first_out, first_tile, ready=None):
                n = first_out + i
                if half == 0:
                    bank_free(sec, n)
                kts = range(half * KT // 2, (half + 1) * KT // 2)
                last = linear(sec, mm[:, n % 2, :], first_tile + i, hid_src, kts, ready=ready)
                if half == 1:
                    last.then_inc(mm_ready, 1)

            def project(sec, i, n, tile, heads=range(HG), tokens=slice(0, CHUNK)):
                if heads[0] == 0:
                    tile_ready(sec, tile)
                    bank_free(sec, n)
                slot = sec.slot(tile)
                for h in heads:
                    col = (i % 2) * HG + h
                    last = product(mm[:, n % 2, tokens], column(slot, 0, col), column(slot, 1, col),
                                   o_t(0, h)[:, tokens], o_t(1, h)[:, tokens], h == 0, h == HG - 1)
                if heads[-1] == HG - 1:
                    last.then_inc(mm_ready, 1)

            def base_and_lora(sec, first_out, first_tile, b_tile, src, hg_k, between=None):
                for i in range(KT):
                    n = first_out + i
                    bank = mm[:, n % 2, :]
                    bank_free(sec, n)
                    if i == 1 and between:
                        linear(sec, bank, first_tile + i, src, range(0, KT // 2), stop=False)
                        between()
                        linear(sec, bank, first_tile + i, src, range(KT // 2, KT), stop=False)
                    else:
                        linear(sec, bank, first_tile + i, src, stop=False)
                    if i == 1:
                        pe.wait_ge(hg_lo, sec.value("hg_lo", hg_k))
                        tile_ready(sec, b_tile)
                        lora(sec, mm[:, (n - 1) % 2, :], 0, n - 1)
                    if i >= 1:
                        lora(sec, bank, i, n)

            def cond(sec):
                pe.wait_ge(gw_lo, 1)
                pe.wait_ge(s_read, sec.value("s_read", 0))
                logits(sec, 0, sc[:, 0, :], xy, lambda kt: pe.wait_ge(x_lo, sec.value("x_lo", kt + 1)))
                linear(sec, sc[:, 1, :], 0, xy).then_inc(s_ready, 1)
                turn_logits(sec, E, 1, 0)
                base_and_lora(sec, 0, 2, 1, xy, 1, lambda: turn_gates(sec, 1))

            def hid_ready(sec, kt):
                pe.wait_ge(mm_read, sec.value("mm_read", kt + 1))

            def first_group(sec):
                for i in range(6):
                    for half in range(2):
                        qkv(sec, i, half, 8, 10, (lambda kt: hid_ready(sec, kt)) if i == 0 else None)
                for n in range(8):
                    scores(sec, n, 2)
                    if n == 1:
                        turn_v(sec, 13, 2)

            def body(sec):
                for step in range(12):
                    qkv(sec, step // 2, step % 2, 0, 0)
                    if 1 <= step <= 6:
                        attend(sec, step - 1)
                    if step <= 5:
                        turn_probs(sec, step)
                pe.wait_ge(o_read, sec.value("o_read", 4))
                for i in range(KT):
                    for half in range(2):
                        project(sec, i, 6 + i, 6 + i // 2, heads=range(2 * half, 2 * half + 2))
                        if 6 <= 2 * i + half < 14:
                            scores(sec, 2 * i + half - 6, 0)
                    if i == 0:
                        turn_v(sec, 5, 6)

            def last_group(sec):
                def first_sample(i):
                    project(sec, i, i, i // 2, tokens=slice(0, SEQ))

                turn_probs(sec, 0, two_banks=True)
                turn_probs(sec, 1, two_banks=True)
                for i in range(3):
                    attend(sec, i)
                    turn_probs(sec, i + 2, two_banks=True)
                pe.wait_ge(o_read, sec.value("o_read", 2))
                first_sample(0)
                attend(sec, 3)
                turn_probs(sec, 5, two_banks=True)
                first_sample(1)
                attend(sec, 4)
                first_sample(2)
                attend(sec, 5)
                for i in range(3, KT):
                    first_sample(i)
                pe.wait_ge(o_read, sec.value("o_read", 4))
                for i in range(KT):
                    project(sec, i, KT + i, i // 2, tokens=slice(SEQ, CHUNK))

            def cond2(sec):
                pe.wait_ge(o_read, sec.value("o_read", 3))
                linear(sec, ob[:, 0, :], 4, hid_src,
                       ready=lambda kt: pe.wait_ge(x1_lo, sec.value("x1_lo", kt + 1))).then_inc(o_ready, 1)
                base_and_lora(sec, 16, 6, 5, hid_src, 1)

            def ffn(sec):
                pe.wait_ge(s_read, sec.value("s_read", 0))
                logits(sec, 1, sc[:, 0, :], xy, lambda kt: pe.wait_ge(mm_read, sec.value("mm_read", 16 + kt + 1)))
                pe.wait_ge(o_read, sec.value("o_read", 4))
                linear(sec, ob[:, 1, :], 14, xy).then_inc(o_ready, 1)
                turn_logits(sec, E + 1, 1, 6)
                base_and_lora(sec, 24, 16, 15, xy, 2, lambda: turn_gates(sec, 7))

            with pe.Fori(0, CHUNKS) as c:
                pre = Section("pre", c)
                cond(pre)
                first_group(pre)
                with pe.Fori(0, BODIES) as g:
                    body(Section("body", c, g))
                post = Section("post", c)
                last_group(post)
                cond2(post)
                ffn(post)

        @block.scalar
        def _(act):
            def split_hi(sec, tile, dst=None):
                s = sec.slot(tile)
                act.wait_ge(w_raw[s], sec.round(tile) * 16)
                nc.scalar.copy(w_sb[:, s, 0, :] if dst is None else dst, w_raw_sb[:, s, :]).then_inc(w_hi[s], 1)

            def rope_swap(sec, n, k):
                s = n % 2
                act.wait_ge(mm_ready, sec.value("mm_ready", n + 1))
                act.wait_ge(rope_lo, sec.value("rope_lo", (0, 0, 1, 2, 3)[k]))
                nc.scalar.copy(swap[0:P // 2, s, :], mm[P // 2:P, s, :])
                nc.scalar.copy(swap[P // 2:P, s, :], mm[0:P // 2, s, :]).then_inc(xs_ready, 1)

            def write_rope_hi(sec, s, k):
                act.wait_ge(rope_sum, sec.value("rope_sum", k + 1))
                dst = k_t[:, 0, :] if k == 0 else q_t(0, k - 1)
                nc.scalar.copy(dst, turn[:, s, :]).then_inc(rope_hi, 1)

            def probs_hi(sec, i, bank=ptb):
                act.wait_ge(ptb_ready, sec.value("ptb_ready", i + 1))
                nc.scalar.copy(p_t[:, i % 2, 0, :], bank[:]).then_inc(ptb_hi, 1)

            def v_hi(sec, ordinal, k):
                act.wait_ge(ptb_ready, sec.value("ptb_ready", ordinal + 1))
                nc.scalar.copy(v_tok[:, 0, :, :], ptb[:].rearrange("p (t d) -> p t d", t=TT)).then_inc(ptb_hi, 1)

            def write_o_hi(sec, n):
                b, qt = n // QT, n % QT
                act.wait_ge(o_ready, sec.value("o_ready", n + 1))
                t0 = b * SEQ + qt * P
                nc.scalar.copy(wide[:, 2, :, t0:t0 + P], ob[:, qt, :].rearrange("p (h t) -> p h t", h=HG)
                               ).then_inc(o_hi, 1)

            def softmax_exp(sec, n):
                b, qt = n // QT, n % QT
                keys = (qt + 1) * P
                act.wait_ge(nmax_ready, sec.value("nmax_ready", n + 1))
                for h in range(HG):
                    pr = probs[:, b, qt, h, 0:keys]
                    last = nc.scalar.activation(pr, pr, ACT.Exp, bias=nmax[:, n, h:h + 1], scale=SCALE,
                                                accum_out=rowsum[:, n, h:h + 1])
                last.then_inc(exp_ready, 1)

            def split_hg():
                nc.scalar.copy(p_t[:, 0, 0, :], hg).then_inc(hg_hi, 1)

            def load_x(sec):
                act.wait_ge(out_stored, sec.c * (16 * KT) + 16)
                for kt in range(KT):
                    act.dma_start(acc[:, kt, :], x_in[bass.ds(sec.c, 1), :, kt, :].rearrange("c p t -> p (c t)")
                                  ).then_inc(x_loaded[kt], 16)

            def cond(sec):
                load_x(sec)
                act.wait_ge(mm_ready, sec.value("mm_ready", 0))
                for kt in range(KT):
                    act.wait_ge(x_loaded[kt], sec.c * 16 + 16)
                    nc.scalar.copy(xy(0, kt), acc[:, kt, :]).then_inc(x_hi, 1)
                for t in (0, 2, 3):
                    split_hi(sec, t)
                act.wait_ge(shift_ready, sec.value("shift_ready", 1))
                nc.scalar.activation(expd, shifted, ACT.Exp).then_inc(gate_exp, 1)
                split_hi(sec, 1, lora_b[:, 0, :])
                split_hi(sec, 4)
                act.wait_ge(s_read, sec.value("s_read", 2))
                split_hg()
                split_hi(sec, 5)
                for i in range(KT):
                    act.wait_ge(mm_ready, sec.value("mm_ready", i + 1))
                    nc.scalar.copy(hid[:, 0, i, :], mm[:, i % 2, :]).then_inc(mm_hi, 1)
                    if i == 0:
                        split_hi(sec, 6)
                    split_hi(sec, 7 + i)

            def first_group(sec):
                rope_swap(sec, 8, 0)
                split_hi(sec, 15)
                write_rope_hi(sec, 0, 0)
                rope_swap(sec, 9, 1)
                split_hi(sec, 16)
                write_rope_hi(sec, 1, 1)
                rope_swap(sec, 10, 2)
                split_hi(sec, 17)
                write_rope_hi(sec, 0, 2)
                rope_swap(sec, 11, 3)
                split_hi(sec, 18)
                write_rope_hi(sec, 1, 3)
                rope_swap(sec, 12, 4)
                split_hi(sec, 19)
                write_rope_hi(sec, 0, 4)
                softmax_exp(sec, 0)
                v_hi(sec, 2, 0)
                softmax_exp(sec, 1)
                softmax_exp(sec, 2)
                softmax_exp(sec, 3)
                split_hi(sec, 20)

            def body(sec):
                probs_hi(sec, 0)
                rope_swap(sec, 0, 0)
                probs_hi(sec, 1)
                write_o_hi(sec, 0)
                split_hi(sec, 5)
                probs_hi(sec, 2)
                write_rope_hi(sec, 0, 0)
                rope_swap(sec, 1, 1)
                probs_hi(sec, 3)
                write_o_hi(sec, 1)
                split_hi(sec, 6)
                probs_hi(sec, 4)
                write_o_hi(sec, 2)
                write_rope_hi(sec, 1, 1)
                rope_swap(sec, 2, 2)
                probs_hi(sec, 5)
                split_hi(sec, 7)
                write_o_hi(sec, 3)
                write_rope_hi(sec, 0, 2)
                rope_swap(sec, 3, 3)
                split_hi(sec, 8)
                write_rope_hi(sec, 1, 3)
                rope_swap(sec, 4, 4)
                split_hi(sec, 9)
                write_rope_hi(sec, 0, 4)
                act.wait_ge(mm_ready, sec.value("mm_ready", 6))
                split_hi(sec, 10)
                v_hi(sec, 6, 0)
                act.wait_ge(mm_ready, sec.value("mm_ready", 8))
                split_hi(sec, 11)
                softmax_exp(sec, 0)
                split_hi(sec, 12)
                softmax_exp(sec, 1)
                softmax_exp(sec, 2)
                act.wait_ge(mm_ready, sec.value("mm_ready", 12))
                split_hi(sec, 13)
                softmax_exp(sec, 3)
                act.wait_ge(mm_ready, sec.value("mm_ready", 14))
                split_hi(sec, 14)

            def last_group(sec):
                for i in range(5):
                    probs_hi(sec, i, (ptb, ptb1)[i % 2])
                    if i in (2, 4):
                        write_o_hi(sec, i // 2 - 1)
                write_o_hi(sec, 2)
                probs_hi(sec, 5, ptb1)
                write_o_hi(sec, 3)
                for i in range(KT):
                    act.wait_ge(mm_read, sec.value("mm_read", KT + i + 1))
                    nc.scalar.copy(hid[:, 0, i, :], acc[:, i, :]).then_inc(x1_hi, 1)
                    if i % 2 == 1 and i >= 3:
                        split_hi(sec, 5 + i // 2)

            def cond2(sec):
                split_hi(sec, 5, lora_b[:, 0, :])
                act.wait_ge(o_read, sec.value("o_read", 5))
                split_hg()
                split_hi(sec, 9)
                for i in range(KT):
                    act.wait_ge(mm_ready, sec.value("mm_ready", 16 + i + 1))
                    nc.scalar.activation(xy(0, i), mm[:, i % 2, :], ACT.Identity, bias=bia[:, B_2 + i:B_2 + i + 1]
                                         ).then_inc(mm_hi, 1)
                    if i == 0:
                        split_hi(sec, 10)
                    if i != 4:
                        split_hi(sec, 11 + i)

            def ffn(sec):
                act.wait_ge(shift_ready, sec.value("shift_ready", 1))
                nc.scalar.activation(expd, shifted, ACT.Exp)
                nc.scalar.activation(thr_e, lg.rearrange("p (t e) -> p t e", t=TT)[:, :, E], ACT.Exp,
                                     bias=neg_bthr[:], scale=-1.0).then_inc(gate_exp, 1)
                split_hi(sec, 15, lora_b[:, 0, :])
                act.wait_ge(o_read, sec.value("o_read", 6))
                split_hg()
                split_hi(sec, 19)
                for i in range(KT):
                    act.wait_ge(mm_ready, sec.value("mm_ready", 24 + i + 1))
                    if i == 0:
                        split_hi(sec, 20)
                    if 21 + i < TILES["post"]:
                        split_hi(sec, 21 + i)
                    act.wait_ge(mm_read, sec.value("mm_read", 24 + i + 1))
                    act.dma_start(out[bass.ds(sec.c, 1), :, i, :].rearrange("c p t -> p (c t)"), acc[:, i, :]
                                  ).then_inc(out_stored, 16)

            act.sem_inc(out_stored, 16)
            act.wait_ge(const_loaded, 16 * N_CONST)
            nc.scalar.copy(gw[:, :, 0, :], gw_raw[:]).then_inc(gw_hi, 1)
            with act.Fori(0, CHUNKS) as c:
                pre = Section("pre", c)
                cond(pre)
                first_group(pre)
                with act.Fori(0, BODIES) as g:
                    body(Section("body", c, g))
                post = Section("post", c)
                last_group(post)
                cond2(post)
                ffn(post)
            act.wait_ge(out_stored, 16 + CHUNKS * 16 * KT)

        @block.gpsimd
        def _(pool):
            def normalise(sec):
                for n in range(CS * QT):
                    b, qt = n // QT, n % QT
                    pool.wait_ge(rsum_ready, sec.value("rsum_ready", n + 1))
                    pool.sem_inc(passed, 1)
                    for h in range(HG):
                        pr = probs[:, b, qt, h, 0:(qt + 1) * P]
                        last = nc.gpsimd.tensor_scalar(pr, pr, rsum[:, n, h:h + 1], 1.0, ALU.mult, ALU.mult)
                    last.then_inc(p_ready, 1)

            def write_rope_sum(sec, k):
                s = k % 2
                pool.wait_ge(t2_ready, sec.value("t2_ready", k + 1))
                nc.gpsimd.tensor_tensor(turn[:, s, :], turn[:, s, :], swap[:, s, :], ALU.add
                                        ).then_inc(rope_sum, 1)

            with pool.Fori(0, CHUNKS) as c:
                pre = Section("pre", c)
                for k in range(5):
                    write_rope_sum(pre, k)
                normalise(pre)
                with pool.Fori(0, BODIES) as g:
                    sec = Section("body", c, g)
                    for k in range(5):
                        write_rope_sum(sec, k)
                    normalise(sec)

        @block.vector
        def _(dve):
            def split_lo(sec, tile, dst=None):
                s = sec.slot(tile)
                dve.wait_ge(w_hi[s], sec.round(tile))
                hi = w_sb[:, s, 0, :] if dst is None else lora_b[:, 0, :]
                lo = w_sb[:, s, 1, :] if dst is None else lora_b[:, 1, :]
                nc.vector.tensor_tensor(lo, w_raw_sb[:, s, :], f(hi), ALU.subtract).then_inc(w_lo[s], 1)

            def rope_products(sec, n, k):
                s = n % 2
                dve.wait_ge(xs_ready, sec.value("xs_ready", k + 1))
                nc.vector.tensor_tensor(by_sample(turn[:, s, :]), by_sample(mm[:, s, :]), cos, ALU.mult
                                        ).then_inc(mm_read, 1)
                nc.vector.tensor_tensor(by_sample(swap[:, s, :]), by_sample(swap[:, s, :]), sin, ALU.mult
                                        ).then_inc(t2_ready, 1)

            def write_rope_lo(sec, s, k):
                dve.wait_ge(rope_hi, sec.value("rope_hi", k + 1))
                hi, lo = (k_t[:, 0, :], k_t[:, 1, :]) if k == 0 else (q_t(0, k - 1), q_t(1, k - 1))
                nc.vector.tensor_tensor(lo, turn[:, s, :], f(hi), ALU.subtract).then_inc(rope_lo, 1)

            def probs_lo(sec, i, bank=ptb):
                dve.wait_ge(ptb_hi, sec.value("ptb_hi", i + 1))
                nc.vector.tensor_tensor(p_t[:, i % 2, 1, :], bank[:], f(p_t[:, i % 2, 0, :]), ALU.subtract
                                        ).then_inc(ptb_read, 1)

            def v_copy(sec, n):
                dve.wait_ge(mm_ready, sec.value("mm_ready", n + 1))
                nc.vector.tensor_copy(v_raw[:], mm[:, n % 2, :]).then_inc(mm_read, 1)

            def v_lo(sec, k):
                dve.wait_ge(ptb_hi, sec.value("ptb_hi", k))
                four = ptb[:].rearrange("p (t d) -> p t d", t=TT)
                nc.vector.tensor_tensor(v_tok[:, 1, :, :], four, f(v_tok[:, 0, :, :]), ALU.subtract
                                        ).then_inc(ptb_read, 1)

            def write_o_lo(sec, n):
                b, qt = n // QT, n % QT
                t0 = b * SEQ + qt * P
                dve.wait_ge(o_hi, sec.value("o_hi", n + 1))
                nc.vector.tensor_tensor(wide[:, 3, :, t0:t0 + P], ob[:, qt, :].rearrange("p (h t) -> p h t", h=HG),
                                        f(wide[:, 2, :, t0:t0 + P]), ALU.subtract).then_inc(o_read, 1)

            def softmax_max(sec, t, first):
                n, pair = t // 2, t % 2
                b, qt = n // QT, n % QT
                keys = (qt + 1) * P
                mask = cst[:, C_MASK + SEQ - keys:C_MASK + SEQ]
                dve.wait_ge(s_ready, sec.value("s_ready", first + t + 1))
                dve.sem_inc(passed, 1)
                for j in range(2):
                    h = 2 * pair + j
                    last = nc.vector.tensor_tensor_reduce(
                        out=probs[:, b, qt, h, 0:keys], in0=sc[:, t % 2, j * SEQ:j * SEQ + keys], in1=mask,
                        scale=1.0, scalar=-3e38, op0=ALU.add, op1=ALU.max, accum_out=rmax[:, n, h:h + 1])
                last.then_inc(s_read, 1)
                if pair == 1:
                    dve.wait_ge(s_read, sec.value("s_read", first + t + 1))
                    nc.vector.tensor_scalar(nmax[:, n, :], rmax[:, n, :], -SCALE, None, ALU.mult
                                            ).then_inc(nmax_ready, 1)

            def softmax_rsum(sec, n):
                dve.wait_ge(exp_ready, sec.value("exp_ready", n + 1))
                nc.vector.reciprocal(rsum[:, n, :], rowsum[:, n, :]).then_inc(rsum_ready, 1)

            def read_logits(sec, rows, ordinal):
                dve.wait_ge(s_ready, sec.value("s_ready", ordinal + 1))
                nc.vector.tensor_copy(logits_t[0:rows, :], sc[0:rows, 0, :]).then_inc(s_read, 1)

            def read_gates(sec, ordinal):
                dve.wait_ge(ptb_ready, sec.value("ptb_ready", ordinal + 1))
                nc.vector.tensor_copy(gates_t, ptb[:]).then_inc(ptb_read, 1)
                dve.wait_ge(ptb_read, sec.value("ptb_read", ordinal + 1))

            def split_hg(sec, k):
                dve.wait_ge(hg_hi, sec.value("hg_hi", k))
                nc.vector.tensor_tensor(p_t[:, 0, 1, :], hg, f(p_t[:, 0, 0, :]), ALU.subtract
                                        ).then_inc(hg_lo, 1)

            class Steps:

                def __init__(self, sec):
                    self.sec, self.n = sec, 0

                def __call__(self, ins):
                    self.n += 1
                    ins.then_inc(gate_step, 1)
                    dve.wait_ge(gate_step, self.sec.value("gate_step", self.n))

            def over_e(ap):
                return ap.rearrange("p (t e) -> p t e", t=TT)

            def per_token(ap):
                return ap[:, :, None].to_broadcast([P, TT, E])

            def spread_gates(step):
                step(nc.vector.scalar_tensor_tensor(out=over_e(gate), in0=over_e(wts), scalar=LORA_SCALE,
                                                    in1=per_token(winv), op0=ALU.mult, op1=ALU.mult))
                nc.vector.tensor_copy(gates_rep.rearrange("p (n r) -> p n r", r=R),
                                      gate[:, :, None].to_broadcast([P, TT * E, R])).then_inc(gates_ready, 1)

            def cond_gates(sec):
                step = Steps(sec)
                lge = over_e(lg[:, 0:TT * E])
                dve.wait_ge(ptb_ready, sec.value("ptb_ready", 1))
                samples = lang_bias[:, bass.ds(sec.c * CS, CS), :]
                nc.vector.tensor_tensor(
                    lg[:, 0:TT * E].rearrange("p (s t e) -> p s t e", s=CS, t=QT),
                    ptb[:, 0:TT * E].rearrange("p (s t e) -> p s t e", s=CS, t=QT),
                    samples[:, :, None, :].to_broadcast([P, CS, QT, E]), ALU.add).then_inc(ptb_read, 1)
                dve.wait_ge(ptb_read, sec.value("ptb_read", 1))
                step(nc.vector.reduce_max(top, lge, AX))
                nc.vector.tensor_tensor(over_e(shifted), lge, per_token(top), ALU.subtract).then_inc(shift_ready, 1)
                pair = lambda ap: ap.rearrange("p (t e o) -> p t e o", t=TT, e=E)
                other = lge[:, :, None, :].to_broadcast([P, TT, E, E])
                own = lge[:, :, :, None].to_broadcast([P, TT, E, E])
                lower = cst[:, None, C_TRI:C_TRI + E * E].to_broadcast([P, TT, E * E])
                step(nc.vector.tensor_tensor(pair(beats), other, own, ALU.is_gt))
                step(nc.vector.tensor_tensor(pair(ties), other, own, ALU.is_equal))
                flat = lambda ap: ap.rearrange("p (t n) -> p t n", t=TT)
                step(nc.vector.tensor_tensor(flat(ties), flat(ties), lower, ALU.mult))
                step(nc.vector.tensor_tensor(beats, beats, ties, ALU.add))
                step(nc.vector.reduce_sum(rank, beats.rearrange("p (n o) -> p n o", o=E), AX))
                step(nc.vector.tensor_scalar(chosen, rank, 1.5, None, ALU.is_lt))
                dve.wait_ge(gate_exp, sec.value("gate_exp", 1))
                step(nc.vector.tensor_tensor(wts, expd, chosen, ALU.mult))
                step(nc.vector.reduce_sum(wsum, over_e(wts), AX))
                step(nc.vector.reciprocal(winv, wsum))
                spread_gates(step)
                assert step.n == COUNTS["gate_step"][0]

            def ffn_gates(sec):
                step = Steps(sec)
                lg9 = lg.rearrange("p (t e) -> p t e", t=TT)
                dve.wait_ge(ptb_ready, sec.value("ptb_ready", 7))
                nc.vector.tensor_copy(lg, ptb[:, 0:TT * (E + 1)]).then_inc(ptb_read, 1)
                dve.wait_ge(ptb_read, sec.value("ptb_read", 7))
                step(nc.vector.reduce_max(top, lg9[:, :, 0:E], AX))
                nc.vector.tensor_tensor(over_e(shifted), lg9[:, :, 0:E], per_token(top), ALU.subtract
                                        ).then_inc(shift_ready, 1)
                dve.wait_ge(gate_exp, sec.value("gate_exp", 1))
                step(nc.vector.reduce_sum(wsum, over_e(expd), AX))
                step(nc.vector.reciprocal(winv, wsum))
                step(nc.vector.tensor_tensor(over_e(rank), over_e(expd), per_token(winv), ALU.mult))
                step(nc.vector.tensor_scalar(thr_1, thr_e, 1.0, None, ALU.add))
                step(nc.vector.reciprocal(thr_r, thr_1))
                step(nc.vector.tensor_scalar(thr, thr_r, MAX_THRESHOLD, None, ALU.mult))
                step(nc.vector.tensor_tensor(over_e(chosen), over_e(rank), per_token(thr), ALU.subtract))
                step(nc.vector.tensor_scalar(wts, chosen, 0.0, None, ALU.max))
                step(nc.vector.reduce_sum(wsum, over_e(wts), AX))
                step(nc.vector.tensor_scalar(is_zero, wsum, 0.0, None, ALU.is_equal))
                step(nc.vector.tensor_tensor(wsum1, wsum, is_zero, ALU.add))
                step(nc.vector.reciprocal(winv, wsum1))
                spread_gates(step)
                assert step.n == COUNTS["gate_step"][2]

            def cond(sec):
                for kt in range(KT):
                    dve.wait_ge(x_hi, sec.value("x_hi", kt + 1))
                    nc.vector.tensor_tensor(xy(1, kt), acc[:, kt, :], f(xy(0, kt)), ALU.subtract
                                            ).then_inc(x_lo, 1)
                for t in (0, 2, 3):
                    split_lo(sec, t)
                read_logits(sec, E, 0)
                cond_gates(sec)
                split_lo(sec, 1, lora_b)
                split_lo(sec, 4)
                read_gates(sec, 1)
                dve.wait_ge(s_ready, sec.value("s_ready", 2))
                nc.vector.tensor_tensor(hg, sc[:, 1, :], gates_t, ALU.mult).then_inc(s_read, 1)
                split_hg(sec, 1)
                split_lo(sec, 5)
                for i in range(KT):
                    dve.wait_ge(mm_hi, sec.value("mm_hi", i + 1))
                    nc.vector.tensor_tensor(hid[:, 1, i, :], mm[:, i % 2, :], f(hid[:, 0, i, :]), ALU.subtract
                                            ).then_inc(mm_read, 1)
                    if i == 0:
                        split_lo(sec, 6)
                    split_lo(sec, 7 + i)

            def first_group(sec):
                rope_products(sec, 8, 0)
                split_lo(sec, 15)
                write_rope_lo(sec, 0, 0)
                rope_products(sec, 9, 1)
                split_lo(sec, 16)
                write_rope_lo(sec, 1, 1)
                rope_products(sec, 10, 2)
                split_lo(sec, 17)
                write_rope_lo(sec, 0, 2)
                rope_products(sec, 11, 3)
                split_lo(sec, 18)
                write_rope_lo(sec, 1, 3)
                rope_products(sec, 12, 4)
                split_lo(sec, 19)
                write_rope_lo(sec, 0, 4)
                v_copy(sec, 13)
                softmax_max(sec, 0, 2)
                softmax_max(sec, 1, 2)
                softmax_max(sec, 2, 2)
                softmax_max(sec, 3, 2)
                v_lo(sec, 1)
                softmax_rsum(sec, 0)
                softmax_max(sec, 4, 2)
                softmax_max(sec, 5, 2)
                softmax_rsum(sec, 1)
                softmax_max(sec, 6, 2)
                softmax_max(sec, 7, 2)
                softmax_rsum(sec, 2)
                softmax_rsum(sec, 3)
                split_lo(sec, 20)

            def body(sec):
                probs_lo(sec, 0)
                rope_products(sec, 0, 0)
                probs_lo(sec, 1)
                write_o_lo(sec, 0)
                split_lo(sec, 5)
                probs_lo(sec, 2)
                write_rope_lo(sec, 0, 0)
                rope_products(sec, 1, 1)
                probs_lo(sec, 3)
                write_o_lo(sec, 1)
                split_lo(sec, 6)
                probs_lo(sec, 4)
                write_o_lo(sec, 2)
                write_rope_lo(sec, 1, 1)
                rope_products(sec, 2, 2)
                probs_lo(sec, 5)
                split_lo(sec, 7)
                write_o_lo(sec, 3)
                write_rope_lo(sec, 0, 2)
                rope_products(sec, 3, 3)
                split_lo(sec, 8)
                write_rope_lo(sec, 1, 3)
                rope_products(sec, 4, 4)
                split_lo(sec, 9)
                write_rope_lo(sec, 0, 4)
                v_copy(sec, 5)
                split_lo(sec, 10)
                add_projection(sec, 0, 6)
                v_lo(sec, 7)
                add_projection(sec, 1, 6)
                split_lo(sec, 11)
                add_projection(sec, 2, 6)
                softmax_max(sec, 0, 0)
                add_projection(sec, 3, 6)
                softmax_max(sec, 1, 0)
                split_lo(sec, 12)
                softmax_max(sec, 2, 0)
                add_projection(sec, 4, 6)
                softmax_max(sec, 3, 0)
                softmax_rsum(sec, 0)
                softmax_max(sec, 4, 0)
                add_projection(sec, 5, 6)
                softmax_max(sec, 5, 0)
                softmax_rsum(sec, 1)
                softmax_max(sec, 6, 0)
                add_projection(sec, 6, 6)
                softmax_max(sec, 7, 0)
                softmax_rsum(sec, 2)
                split_lo(sec, 13)
                add_projection(sec, 7, 6)
                softmax_rsum(sec, 3)
                split_lo(sec, 14)

            def add_projection(sec, i, first_out, tokens=slice(0, CHUNK)):
                n = first_out + i
                dve.wait_ge(mm_ready, sec.value("mm_ready", n + 1))
                nc.vector.tensor_tensor(acc[:, i, tokens], mm[:, n % 2, tokens], acc[:, i, tokens], ALU.add
                                        ).then_inc(mm_read, 1)

            def last_group(sec):
                for i in range(5):
                    probs_lo(sec, i, (ptb, ptb1)[i % 2])
                    if i in (2, 4):
                        write_o_lo(sec, i // 2 - 1)
                add_projection(sec, 0, 0, slice(0, SEQ))
                write_o_lo(sec, 2)
                probs_lo(sec, 5, ptb1)
                add_projection(sec, 1, 0, slice(0, SEQ))
                add_projection(sec, 2, 0, slice(0, SEQ))
                write_o_lo(sec, 3)
                for i in range(3, KT):
                    add_projection(sec, i, 0, slice(0, SEQ))
                for i in range(KT):
                    add_projection(sec, i, KT, slice(SEQ, CHUNK))
                    dve.wait_ge(x1_hi, sec.value("x1_hi", i + 1))
                    nc.vector.tensor_tensor(hid[:, 1, i, :], acc[:, i, :], f(hid[:, 0, i, :]), ALU.subtract
                                            ).then_inc(x1_lo, 1)
                    if i % 2 == 1 and i >= 3:
                        split_lo(sec, 5 + i // 2)

            def cond2(sec):
                split_lo(sec, 5, lora_b)
                dve.wait_ge(o_ready, sec.value("o_ready", 5))
                for s in range(CS):
                    own = cst[:, bass.ds(sec.c * CS + (C_OWN + s), 1)]
                    last = nc.vector.tensor_scalar(hg[:, s * SEQ:(s + 1) * SEQ], ob[:, 0, s * SEQ:(s + 1) * SEQ],
                                                   own, None, ALU.mult)
                last.then_inc(o_read, 1)
                split_hg(sec, 1)
                split_lo(sec, 9)
                for i in range(KT):
                    dve.wait_ge(mm_hi, sec.value("mm_hi", i + 1))
                    nc.vector.scalar_tensor_tensor(out=xy(1, i), in0=mm[:, i % 2, :],
                                                   scalar=bia[:, B_2 + i:B_2 + i + 1], in1=f(xy(0, i)),
                                                   op0=ALU.add, op1=ALU.subtract).then_inc(mm_read, 1)
                    if i == 0:
                        split_lo(sec, 10)
                    if i != 4:
                        split_lo(sec, 11 + i)

            def ffn(sec):
                read_logits(sec, E + 1, 0)
                ffn_gates(sec)
                split_lo(sec, 15, lora_b)
                read_gates(sec, 7)
                dve.wait_ge(o_ready, sec.value("o_ready", 6))
                nc.vector.tensor_tensor(hg, ob[:, 1, :], gates_t, ALU.mult).then_inc(o_read, 1)
                split_hg(sec, 2)
                split_lo(sec, 19)
                for i in range(KT):
                    dve.wait_ge(mm_ready, sec.value("mm_ready", 24 + i + 1))
                    nc.vector.scalar_tensor_tensor(out=acc[:, i, :], in0=mm[:, i % 2, :],
                                                   scalar=bia[:, B_B + i:B_B + i + 1], in1=acc[:, i, :],
                                                   op0=ALU.add, op1=ALU.add).then_inc(mm_read, 1)
                    if i == 0:
                        split_lo(sec, 20)
                    if 21 + i < TILES["post"]:
                        split_lo(sec, 21 + i)

            done = [0]

            def link(ins):
                done[0] += 1
                ins.then_inc(setup, 1)
                dve.wait_ge(setup, done[0])

            dve.wait_ge(const_loaded, 16 * N_CONST)
            link(nc.vector.tensor_copy(ids_f[:], ids_raw[:]))
            link(nc.vector.tensor_scalar(slot_neg[:], ids_f[:, 1, :], 0.0, float(SLOTS), ALU.is_lt, ALU.mult))
            link(nc.vector.tensor_tensor(ids_f[:, 1, :], ids_f[:, 1, :], slot_neg[:], ALU.add))
            link(nc.vector.tensor_scalar(slot_neg[:], ids_f[:, 1, :], 0.0, float(SLOTS - 1), ALU.max, ALU.min))
            nc.vector.tensor_copy(slot_ids[:], slot_neg[:]).then_inc(slots_ready, 1)
            iota = cst[:, None, C_IOTA:C_IOTA + E].to_broadcast([P, SAMPLES, E])
            lang = ids_f[:, 0, :, None].to_broadcast([P, SAMPLES, E])
            link(nc.vector.tensor_tensor(lang_bias[:], iota, lang, ALU.is_equal))
            link(nc.vector.tensor_scalar(lang_bias[:], lang_bias[:], LANG_BIAS, None, ALU.mult))
            link(nc.vector.tensor_scalar(neg_bthr[:], bia[:, B_THR:B_THR + 1], -1.0, None, ALU.mult))
            dve.wait_ge(gw_hi, 1)
            nc.vector.tensor_tensor(gw[:, :, 1, :], gw_raw[:], f(gw[:, :, 0, :]), ALU.subtract).then_inc(gw_lo, 1)
            with dve.Fori(0, CHUNKS) as c:
                pre = Section("pre", c)
                cond(pre)
                first_group(pre)
                with dve.Fori(0, BODIES) as g:
                    body(Section("body", c, g))
                post = Section("post", c)
                last_group(post)
                cond2(post)
                ffn(post)


def shape_constants():
    f32 = np.float32
    inv_freq = (f32(1.0) / f32(10000.0) ** (np.arange(0, HD, 2, dtype=f32) / f32(HD))).astype(f32)
    freqs = np.outer(np.arange(SEQ, dtype=f32), inv_freq).astype(f32).T
    c = np.zeros((P, C_COLS), f32)
    c[:, C_COS:C_COS + SEQ] = np.concatenate([np.cos(freqs), np.cos(freqs)])
    c[:, C_SIN:C_SIN + SEQ] = np.concatenate([-np.sin(freqs), np.sin(freqs)])
    q, k = np.arange(P)[:, None], np.arange(P)[None, :]
    c[:, C_MASK + P:C_MASK + 2 * P] = np.where(k > q, f32(MASKED), f32(0))
    c[:, C_ID:C_ID + P] = np.eye(P, dtype=f32)
    c[:, C_TRI:C_TRI + E * E] = (np.arange(E)[None, :] < np.arange(E)[:, None]).astype(f32).reshape(1, -1)
    c[:, C_IOTA:C_IOTA + E] = np.arange(E, dtype=f32)
    c[:, C_OWN:C_OWN + SAMPLES] = np.where(np.arange(P)[:, None] // R == np.arange(SAMPLES), f32(LORA_SCALE), f32(0))
    return c


def weight_tiles(i):
    def rows(w):
        return w.reshape(-1, P, KT, P).transpose(0, 3, 2, 1).reshape(-1, P, D)

    def lora_a(a):
        return rows(a.reshape(E * R, D))

    def lora_b(b):
        return b.transpose(0, 2, 1).reshape(1, E * R, D)

    wqkv = rows(i["L0_attn_Wqkv"])
    order = [[HEADS + g] + [HG * g + h for h in range(HG)] + [HEADS + KV + g] for g in range(KV)]
    wo = i["L0_attn_Wo"].reshape(KT // 2, 2, P, KV, HG, HD).transpose(3, 0, 5, 1, 4, 2).reshape(KV, KT // 2, P, D)
    parts = [lora_a(i["L0_cond_A"]), lora_b(i["L0_cond_B"]), rows(i["L0_cond_W"]), wqkv[order[0]]]
    for g in range(BODIES):
        parts += [wqkv[order[g + 1]], wo[g]]
    parts += [wo[KV - 1], rows(i["L0_cond2_W"]), lora_a(i["L0_ffn_A_w"]), lora_b(i["L0_ffn_B_w"]),
              rows(i["L0_ffn_W_base"])]
    return np.ascontiguousarray(np.concatenate(parts))


def kernel(**inputs):
    import concourse.bacc as bacc
    from concourse.bass_utils import run_bass_kernel_spmd

    i = {k: np.asarray(v) for k, v in inputs.items()}
    f32 = np.float32
    x = i["x"].reshape(CHUNKS, CHUNK, KT, P).transpose(0, 3, 2, 1)
    gate_w = np.zeros((P, 2, WG_COLS), f32)
    wr = i["L0_cond_Wr"].reshape(E, KT, P)
    wg = np.concatenate([i["L0_ffn_W_gate"], i["L0_ffn_W_thr"][None]]).reshape(E + 1, KT, P)
    for kt in range(KT):
        gate_w[:, 0, kt * WG_STEP:kt * WG_STEP + E] = wr[:, kt].T
        gate_w[:, 1, kt * WG_STEP:kt * WG_STEP + E + 1] = wg[:, kt].T
    biases = np.concatenate([i["L0_cond2_b"].reshape(KT, P).T, i["L0_ffn_b_base"].reshape(KT, P).T,
                             np.broadcast_to(i["L0_ffn_b_thr"], (P, 1))], axis=1)
    ids = np.broadcast_to(np.stack([i["itok_B_0_7"], i["itok_B_0_23"]]), (P, 2, SAMPLES))
    arrays = {
        "x": x,
        "stream": weight_tiles(i),
        "adapters_a": i["L0_cond2_lora_As"].reshape(SLOTS, KT, P, R).transpose(0, 2, 1, 3),
        "adapters_b": i["L0_cond2_lora_Bs"],
        "gate_w": gate_w,
        "consts": shape_constants(),
        "biases": biases,
        "ids": ids,
    }
    arrays = {k: np.ascontiguousarray(v) for k, v in arrays.items()}
    nc = bacc.Bacc("TRN2", target_bir_lowering=False, num_devices=1)
    args = [nc.dram_tensor(k, a.shape, mybir.dt.from_np(a.dtype), kind="ExternalInput").ap()
            for k, a in arrays.items()]
    out = nc.dram_tensor("out", (CHUNKS, P, KT, CHUNK), F32, kind="ExternalOutput").ap()
    build(nc, *args, out)
    got = run_bass_kernel_spmd(nc, [arrays], core_ids=[0]).results[0]["out"]
    return got.transpose(0, 3, 2, 1).reshape(SAMPLES, SEQ, D)
```

```python
from contextlib import ExitStack

import numpy as np
import concourse.bass as bass
from concourse import mybir

F32 = mybir.dt.float32
F32R = mybir.dt.float32r
I32 = mybir.dt.int32
ALU = mybir.AluOpType
ACT = mybir.ActivationFunctionType
AX = mybir.AxisListType.X

P = 128
SAMPLES, SEQ, D = 8, 256, 1024
KT = D // P
CHUNK = 512
CHUNKS = SAMPLES * SEQ // CHUNK
CS = CHUNK // SEQ
TT = CHUNK // P
HEADS, KV, HD = 32, 8, 128
HG = HEADS // KV
QT = SEQ // P
E, R = 8, 16
SLOTS = 32
OWN = CS * R
SCALE = float(1.0 / np.sqrt(np.float32(HD)))
MASKED = -1e30
LANG_BIAS = 5.0
LORA_SCALE = 2.0
MAX_THRESHOLD = 0.125

RING = 5
TILES = {"pre": 16, "body": 10, "post": 24}
BODIES = KV - 1
TILES_CHUNK = TILES["pre"] + BODIES * TILES["body"] + TILES["post"]
AHEAD = (0, 1, 2, 3, 5, 6)
GATHER_AT = 90
assert TILES_CHUNK % RING == 0 and TILES["body"] % RING == 0 and GATHER_AT % RING == 0

COUNTS = {
    "mm_ready":   (14, 14, 32, 1),
    "mm_hi":      (8, 0, 8, 0),
    "mm_read":    (14, 14, 32, 2),
    "s_ready":    (10, 8, 1, 0),
    "s_read":     (10, 8, 1, 1),
    "ptb_ready":  (3, 7, 8, 0),
    "ptb_hi":     (1, 7, 6, 0),
    "ptb_read":   (3, 7, 8, 1),
    "o_ready":    (0, 4, 6, 0),
    "o_hi":       (0, 4, 4, 0),
    "o_read":     (0, 4, 6, 2),
    "low_ready":  (4, 4, 0, 0),
    "nmax_ready": (4, 4, 0, 0),
    "exp_ready":  (4, 4, 0, 0),
    "rsum_ready": (4, 4, 0, 0),
    "p_ready":    (4, 4, 0, 0),
    "xs_ready":   (5, 5, 0, 0),
    "t2_ready":   (5, 5, 0, 0),
    "rope_sum":   (5, 5, 0, 0),
    "rope_hi":    (5, 5, 0, 0),
    "rope_lo":    (5, 5, 0, 1),
    "x_hi":       (0, 0, 8, 8),
    "x_lo":       (0, 0, 8, 8),
    "x1_hi":      (0, 0, 16, 0),
    "x1_lo":      (0, 0, 16, 0),
    "shift_ready": (1, 0, 1, 0),
    "gate_exp":   (1, 0, 1, 0),
    "gate_step":  (12, 0, 15, 0),
    "gates_ready": (1, 0, 1, 0),
    "own_low":    (0, 0, 1, 0),
    "hg_hi":      (1, 0, 2, 0),
    "hg_lo":      (1, 0, 2, 0),
}

C_COS, C_SIN, C_MASK, C_ID, C_TRI, C_IOTA, C_OWN = 0, 256, 512, 768, 896, 960, 968
C_COLS = C_OWN + CS
B_2, B_B, B_THR = 0, KT, 2 * KT
WG_STEP, WG_LO = 32, 16
WG_COLS = (KT - 1) * WG_STEP + P


class Section:

    def __init__(self, kind, c, g=0):
        self.kind, self.c, self.g = kind, c, g

    def count(self, pre, body, post, k):
        per_chunk = pre + BODIES * body + post
        if self.kind == "pre":
            return self.c * per_chunk + k
        if self.kind == "body":
            return self.c * per_chunk + self.g * body + (pre + k)
        return self.c * per_chunk + (pre + BODIES * body + k)

    def value(self, name, k):
        pre, body, post, at_start = COUNTS[name]
        return self.count(pre, body, post, k + at_start)

    def slot(self, tile):
        before = {"pre": 0, "body": TILES["pre"], "post": TILES["pre"] + BODIES * TILES["body"]}[self.kind]
        return (before + tile) % RING

    def round(self, tile):
        before = {"pre": 0, "body": TILES["pre"], "post": TILES["pre"] + BODIES * TILES["body"]}[self.kind]
        turns = (before + tile) // RING + 1
        per_chunk, per_body = TILES_CHUNK // RING, TILES["body"] // RING
        if self.kind == "body":
            return self.c * per_chunk + self.g * per_body + turns
        return self.c * per_chunk + turns


def build(nc, x_in, stream, adapters_a, adapters_b, gate_w, consts, biases, ids, out):
    ctx = ExitStack()
    with ctx:
        def sb(name, shape, dt=F32):
            return ctx.enter_context(nc.sbuf_tensor(name, shape, dt))

        def psum(name, shape):
            return ctx.enter_context(nc.psum_tensor(name, shape, F32))

        gathered_a = nc.dram_tensor("gathered_a", (CHUNKS, P, KT, CS, R), F32, kind="Internal").ap()
        gathered_b = nc.dram_tensor("gathered_b", (CHUNKS, 3, CS, R, D), F32, kind="Internal").ap()

        hid = sb("hid", [P, 2, KT, CHUNK], F32R)
        wide = sb("wide", [P, 4, HG, CHUNK], F32R)
        acc = sb("acc", [P, KT, CHUNK])
        k_t = sb("k_t", [P, 2, CHUNK], F32R)
        v_tok = sb("v_tok", [P, 2, TT, HD], F32R)
        v_raw = sb("v_raw", [P, CHUNK])
        probs = sb("probs", [P, CS, QT, HG, SEQ])
        p_t = sb("p_t", [P, 2, 2, CHUNK], F32R)
        w_raw_sb = sb("w_raw_sb", [P, RING, D])
        w_sb = sb("w_sb", [P, RING, 2, D], F32R)
        lora_b = sb("lora_b", [P, 2, D], F32R)
        swap = sb("swap", [P, 2, CHUNK])
        turn = sb("turn", [P, 2, CHUNK])
        gw_raw = sb("gw_raw", [P, 2, WG_COLS])
        gw = sb("gw", [P, 2, WG_COLS], F32R)
        cst = sb("cst", [P, C_COLS])
        bia = sb("bia", [P, 2 * KT + 1])
        neg_bthr = sb("neg_bthr", [P, 1])
        ids_raw = sb("ids_raw", [P, 2, SAMPLES], I32)
        ids_f = sb("ids_f", [P, 2, SAMPLES])
        slot_neg = sb("slot_neg", [P, SAMPLES])
        slot_ids = sb("slot_ids", [P, SAMPLES], I32)
        lang_bias = sb("lang_bias", [P, SAMPLES, E])
        rmax = sb("rmax", [P, 4, HG])
        nmax = sb("nmax", [P, 4, HG])
        rowsum = sb("rowsum", [P, 4, HG])
        rsum = sb("rsum", [P, 4, HG])

        scratch = probs[:].rearrange("p a b c d -> p (a b c d)")
        logits_t = scratch[:, 0:512]
        gates_t = scratch[:, 512:1024]
        gates_rep = scratch[:, 1024:1536]
        hg = logits_t
        beats, ties = gates_t[:, 0:256], gates_t[:, 256:512]
        small = scratch[:, 1536:1536 + 16 * 40]
        spare = scratch[:, 1536 + 16 * 40:]
        lg = small[:, 0:36]
        shifted = small[:, 40:72]
        expd = small[:, 80:112]
        rank = small[:, 120:152]
        chosen = small[:, 160:192]
        wts = small[:, 200:232]
        gate = small[:, 240:272]
        top = small[:, 280:284]
        wsum = small[:, 320:324]
        winv = small[:, 360:364]
        thr_e = small[:, 400:404]
        thr_1 = small[:, 440:444]
        thr_r = small[:, 480:484]
        thr = small[:, 520:524]
        is_zero = small[:, 560:564]
        wsum1 = small[:, 600:604]

        mm = psum("mm", [P, 2, 512])
        sc = psum("sc", [P, 2, 512])
        ptb = psum("ptb", [P, 512])
        ptb1 = psum("ptb1", [P, 512])
        ob = psum("ob", [P, 2, 512])

        def semaphore(name):
            return ctx.enter_context(nc.semaphore(name))

        mm_ready = semaphore("mm_ready")
        mm_hi = semaphore("mm_hi")
        mm_read = semaphore("mm_read")
        s_ready = semaphore("s_ready")
        s_read = semaphore("s_read")
        ptb_ready = semaphore("ptb_ready")
        ptb_hi = semaphore("ptb_hi")
        ptb_read = semaphore("ptb_read")
        o_ready = semaphore("o_ready")
        o_hi = semaphore("o_hi")
        o_read = semaphore("o_read")
        low_ready = semaphore("low_ready")
        nmax_ready = semaphore("nmax_ready")
        exp_ready = semaphore("exp_ready")
        rsum_ready = semaphore("rsum_ready")
        p_ready = semaphore("p_ready")
        xs_ready = semaphore("xs_ready")
        t2_ready = semaphore("t2_ready")
        rope_sum = semaphore("rope_sum")
        rope_hi = semaphore("rope_hi")
        rope_lo = semaphore("rope_lo")
        x_hi = semaphore("x_hi")
        x_lo = semaphore("x_lo")
        x1_hi = semaphore("x1_hi")
        x1_lo = semaphore("x1_lo")
        shift_ready = semaphore("shift_ready")
        gate_exp = semaphore("gate_exp")
        gate_step = semaphore("gate_step")
        gates_ready = semaphore("gates_ready")
        own_low = semaphore("own_low")
        hg_hi = semaphore("hg_hi")
        hg_lo = semaphore("hg_lo")
        w_raw = [semaphore(f"w_raw{s}") for s in range(RING)]
        w_hi = [semaphore(f"w_hi{s}") for s in range(RING)]
        w_lo = [semaphore(f"w_lo{s}") for s in range(RING)]
        x_staged = [semaphore(f"x_staged{k}") for k in range(KT)]
        acc_loaded = semaphore("acc_loaded")
        out_stored = semaphore("out_stored")
        const_loaded = semaphore("const_loaded")
        gw_loaded = semaphore("gw_loaded")
        ids_loaded = semaphore("ids_loaded")
        slots_ready = semaphore("slots_ready")
        adapters_ready = semaphore("adapters_ready")
        gw_hi = semaphore("gw_hi")
        gw_lo = semaphore("gw_lo")
        setup = semaphore("setup")
        passed = semaphore("passed")
        N_CONST = 2

        def f(ap):
            return ap.bitcast(F32)

        cos = cst[:, None, C_COS:C_COS + SEQ].to_broadcast([P, CS, SEQ])
        sin = cst[:, None, C_SIN:C_SIN + SEQ].to_broadcast([P, CS, SEQ])
        ident = cst[:, C_ID:C_ID + P]

        def by_sample(ap):
            return ap.rearrange("p (s t) -> p s t", s=CS)

        def y1(hl, kt):
            return wide[:, 2 * hl + kt // HG, kt % HG, :]

        def x_t(hl, kt):
            if kt == 0:
                return p_t[:, 1, hl, :]
            if kt == 1:
                return k_t[:, hl, :]
            if kt == 2:
                return v_tok[:, hl, :, :].rearrange("p t d -> p (t d)")
            return wide[:, 2 * hl + kt // HG, kt % HG, :]

        def staged(kt):
            if kt < 4:
                return (swap, turn)[kt // 2][:, kt % 2, :]
            if kt == 4:
                return v_raw[:]
            return spare[:, (kt - 5) * CHUNK:(kt - 4) * CHUNK]

        def lin_bank(i):
            return (mm[:, 0, :], mm[:, 1, :], ptb1[:])[i % 3]

        def q_t(hl, h):
            return wide[:, hl, h, :]

        def o_t(hl, h):
            return wide[:, 2 + hl, h, :]

        def own_a(s, part):
            if part == "raw":
                return w_raw_sb[:, s, 0:KT * OWN].rearrange("p (k n) -> p k n", k=KT)
            both = w_sb[:, s, 0, 0:KT * 2 * OWN].rearrange("p (k hl n) -> p k hl n", k=KT, hl=2)
            return both[:, :, 0 if part == "hi" else 1, :]

        block = ctx.enter_context(nc.Block())

        @block.sync
        def _(sp):
            sp.dma_start(w_raw_sb[:, 0, :], stream[0]).then_inc(w_raw[0], 16)
            sp.dma_start(ids_raw[:], ids).then_inc(ids_loaded, 16)
            sp.dma_start(gw_raw[:], gate_w).then_inc(gw_loaded, 16)
            sp.dma_start(cst[:], consts).then_inc(const_loaded, 16)
            sp.dma_start(bia[:], biases).then_inc(const_loaded, 16)
            for t in (2, 3, 1, 4):
                sp.dma_start(w_raw_sb[:, t, :], stream[t]).then_inc(w_raw[t], 16)
            sp.wait_ge(slots_ready, 1)
            for b in range(SAMPLES):
                a = sp.value_load(slot_ids[0:1, b:b + 1], min_val=0, max_val=SLOTS - 1)
                sp.dma_start(gathered_a[b // CS, :, :, b % CS, :],
                             adapters_a[bass.ds(a, 1)].rearrange("s p k r -> p (s k) r")
                             ).then_inc(adapters_ready, 16)
                for copy in range(3):
                    sp.dma_start(gathered_b[b // CS, copy, b % CS], adapters_b[bass.ds(a, 1)].rearrange("s r d -> (s r) d")
                                 ).then_inc(adapters_ready, 16)
            rounds = TILES_CHUNK // RING

            def load(c, i, s, src, dst=None):
                sp.wait_ge(w_lo[s], c * rounds + i + 1)
                sp.dma_start(w_raw_sb[:, s, :] if dst is None else dst, src).then_inc(w_raw[s], 16)

            def tile_of_stream(n):
                return stream[bass.ds(n, 1)].rearrange("n p d -> (n p) d")

            with sp.Fori(0, CHUNKS) as c:
                with sp.Fori(1, GATHER_AT // RING) as i:
                    for s in range(RING):
                        load(c, i, s, tile_of_stream(i * RING + s))
                sp.wait_ge(adapters_ready, 16 * 4 * SAMPLES)
                load(c, GATHER_AT // RING, 0, gathered_a[bass.ds(c, 1)].rearrange("c p k b r -> p (c k b r)"),
                     w_raw_sb[:, 0, 0:KT * OWN])
                load(c, GATHER_AT // RING, 1, gathered_b[bass.ds(c, 1)].rearrange("c n b r d -> (c n b r) d"),
                     w_raw_sb[0:3 * OWN, 1, :])
                for s in range(2, RING):
                    load(c, GATHER_AT // RING, s, stream[GATHER_AT + s - 2])
                with sp.Fori(GATHER_AT // RING + 1, rounds) as i:
                    for s in range(RING):
                        load(c, i, s, tile_of_stream(i * RING + (s - 2)))
                for s in range(RING):
                    load(c, rounds, s, stream[s])
            for s in range(RING):
                sp.wait_ge(w_raw[s], 16 * (CHUNKS * rounds + 1))

        @block.tensor
        def _(pe):
            for s in range(RING):
                pe.sem_inc(w_lo[s], 1)
            pe.sem_inc(mm_ready, COUNTS["mm_ready"][3])
            pe.sem_inc(mm_read, COUNTS["mm_read"][3])
            pe.sem_inc(s_read, COUNTS["s_read"][3])
            pe.sem_inc(ptb_read, COUNTS["ptb_read"][3])
            pe.sem_inc(o_read, COUNTS["o_read"][3])
            pe.sem_inc(rope_lo, COUNTS["rope_lo"][3])

            def product(bank, w_hi_ap, w_lo_ap, x_hi_ap, x_lo_ap, start, stop):
                nc.tensor.matmul(bank, w_hi_ap, x_hi_ap, start=start, stop=False, skip_group_check=True)
                nc.tensor.matmul(bank, w_hi_ap, x_lo_ap, start=False, stop=False, skip_group_check=True)
                return nc.tensor.matmul(bank, w_lo_ap, x_hi_ap, start=False, stop=stop, skip_group_check=True)

            def two_products(bank, hi, lo, both):
                nc.tensor.matmul(bank, hi, both, start=True, stop=False, skip_group_check=True)
                return nc.tensor.matmul(bank, lo, both, start=False, stop=True, skip_group_check=True)

            def tile_ready(sec, tile):
                pe.wait_ge(w_lo[sec.slot(tile)], sec.round(tile) + 1)

            def column(slot, hl, n):
                return w_sb[:, slot, hl, n * P:(n + 1) * P]

            def linear(sec, bank, tile, src, kts=range(KT), stop=True, ready=None):
                slot = sec.slot(tile)
                if kts[0] == 0:
                    tile_ready(sec, tile)
                for kt in kts:
                    if ready:
                        ready(kt)
                    last = product(bank, column(slot, 0, kt), column(slot, 1, kt), src(0, kt), src(1, kt),
                                   kt == 0, stop and kt == KT - 1)
                return last

            def hid_src(hl, kt):
                return hid[:, hl, kt, :]

            def logits(sec, which, bank, src):
                for kt in range(KT):
                    cols = slice(kt * WG_STEP, kt * WG_STEP + P)
                    nc.tensor.matmul(bank, gw[:, which, cols], src(0, kt), start=kt == 0, stop=False,
                                     skip_group_check=True)
                    last = nc.tensor.matmul(bank, gw[:, which, cols], src(1, kt), start=False, stop=kt == KT - 1,
                                            skip_group_check=True)
                last.then_inc(s_ready, 1)

            def lora(sec, bank, i):
                product(bank, lora_b[:, 0, i * P:(i + 1) * P], lora_b[:, 1, i * P:(i + 1) * P],
                        p_t[:, 0, 0, :], p_t[:, 0, 1, :], False, True).then_inc(mm_ready, 1)

            def own_lora(sec, bank, i):
                nc.tensor.matmul(bank, lora_b[0:3 * OWN, 0, i * P:(i + 1) * P], p_t[0:3 * OWN, 0, 0, :],
                                 start=False, stop=True, skip_group_check=True).then_inc(mm_ready, 1)

            def turn_logits(sec, read_k, ordinal):
                rows = 2 * WG_LO
                pe.wait_ge(s_read, sec.value("s_read", read_k))
                pe.wait_ge(ptb_read, sec.value("ptb_read", ordinal))
                pe.sem_inc(passed, 1)
                for t in range(TT):
                    last = nc.tensor.transpose(ptb[:, t * rows:(t + 1) * rows], logits_t[0:rows, t * P:(t + 1) * P],
                                               cst[0:rows, C_ID:C_ID + rows])
                last.then_inc(ptb_ready, 1)

            def turn_gates(sec, ordinal):
                pe.wait_ge(gates_ready, sec.value("gates_ready", 1))
                pe.wait_ge(ptb_read, sec.value("ptb_read", ordinal))
                for t in range(TT):
                    last = nc.tensor.transpose(ptb[:, t * P:(t + 1) * P], gates_rep[:, t * P:(t + 1) * P], ident)
                last.then_inc(ptb_ready, 1)

            def scores(sec, n, first):
                b, qt, pair = n // 4, n // 2 % 2, n % 2
                if n == 0:
                    pe.wait_ge(rope_lo, sec.value("rope_lo", 5))
                pe.wait_ge(s_read, sec.value("s_read", first + n - 1))
                for j in range(2):
                    h = 2 * pair + j
                    q0 = b * SEQ + qt * P
                    bank = sc[:, n % 2, j * SEQ:(j + 1) * SEQ]
                    if qt == 0:
                        keys = k_t[:, :, b * SEQ:b * SEQ + P]
                        last = two_products(bank.rearrange("p (hl k) -> p hl k", hl=2),
                                            q_t(0, h)[:, q0:q0 + P], q_t(1, h)[:, q0:q0 + P], keys)
                    else:
                        last = product(bank, q_t(0, h)[:, q0:q0 + P], q_t(1, h)[:, q0:q0 + P],
                                       k_t[:, 0, b * SEQ:(b + 1) * SEQ], k_t[:, 1, b * SEQ:(b + 1) * SEQ], True, True)
                last.then_inc(s_ready, 1)

            BLOCKS = [(0, 0), (0, 1), (1, 1)]

            def turn_probs(sec, i, two_banks=False):
                b, (kt, qt) = i // 3, BLOCKS[i % 3]
                bank = ptb1 if two_banks and i % 2 else ptb
                pe.wait_ge(p_ready, sec.value("p_ready", b * QT + qt + 1 - CS * QT))
                pe.wait_ge(ptb_read, sec.value("ptb_read", max(i - 1, 0) if two_banks else i))
                for h in range(HG):
                    last = nc.tensor.transpose(bank[:, h * P:(h + 1) * P], probs[:, b, qt, h, kt * P:(kt + 1) * P],
                                               ident)
                last.then_inc(ptb_ready, 1)

            def attend(sec, i):
                b, (kt, qt) = i // 3, BLOCKS[i % 3]
                pe.wait_ge(ptb_read, sec.value("ptb_read", i + 1))
                if kt == 0:
                    pe.wait_ge(o_read, sec.value("o_read", b * QT + qt - 1))
                last = product(ob[:, qt, :], v_tok[:, 0, b * QT + kt, :], v_tok[:, 1, b * QT + kt, :],
                               p_t[:, i % 2, 0, :], p_t[:, i % 2, 1, :], kt == 0, kt == qt)
                if kt == qt:
                    last.then_inc(o_ready, 1)

            def turn_v(sec, out_n, ordinal):
                pe.wait_ge(mm_read, sec.value("mm_read", out_n + 1))
                pe.wait_ge(ptb_read, sec.value("ptb_read", ordinal))
                for t in range(TT):
                    last = nc.tensor.transpose(ptb[:, t * P:(t + 1) * P], v_raw[:, t * P:(t + 1) * P], ident)
                last.then_inc(ptb_ready, 1)

            def bank_free(sec, n):
                pe.wait_ge(mm_read, sec.value("mm_read", n - 1))

            def qkv(sec, i, half, first_out, first_tile, ready=None):
                n = first_out + i
                if half == 0:
                    bank_free(sec, n)
                kts = range(half * KT // 2, (half + 1) * KT // 2)
                last = linear(sec, mm[:, n % 2, :], first_tile + i, hid_src, kts, ready=ready)
                if half == 1:
                    last.then_inc(mm_ready, 1)

            def project(sec, i, n, tile, heads=range(HG), tokens=slice(0, CHUNK)):
                if heads[0] == 0:
                    tile_ready(sec, tile)
                    bank_free(sec, n)
                slot = sec.slot(tile)
                for h in heads:
                    col = (i % 2) * HG + h
                    last = product(mm[:, n % 2, tokens], column(slot, 0, col), column(slot, 1, col),
                                   o_t(0, h)[:, tokens], o_t(1, h)[:, tokens], h == 0, h == HG - 1)
                if heads[-1] == HG - 1:
                    last.then_inc(mm_ready, 1)

            def base_and_lora(sec, first_out, first_tile, b_tile, src, hg_k, lora, between):
                for i in range(KT):
                    n = first_out + i
                    pe.wait_ge(mm_read, sec.value("mm_read", n - 1 if i < 2 else n - 2))
                    if i in between:
                        linear(sec, lin_bank(i), first_tile + i, src, range(0, KT // 2), stop=False)
                        between[i]()
                        linear(sec, lin_bank(i), first_tile + i, src, range(KT // 2, KT), stop=False)
                    else:
                        linear(sec, lin_bank(i), first_tile + i, src, stop=False)
                    if i == 2:
                        pe.wait_ge(hg_lo, sec.value("hg_lo", hg_k))
                        tile_ready(sec, b_tile)
                        lora(sec, lin_bank(0), 0)
                        lora(sec, lin_bank(1), 1)
                    if i >= 2:
                        lora(sec, lin_bank(i), i)

            def cond(sec):
                pe.wait_ge(s_read, sec.value("s_read", 0))
                linear(sec, sc[:, 1, :], 0, x_t, ready=lambda kt: pe.wait_ge(x_lo, sec.value("x_lo", kt + 1 - KT))
                       ).then_inc(s_ready, 1)
                pe.wait_ge(gw_lo, 1)
                logits(sec, 0, sc[:, 0, :], x_t)
                base_and_lora(sec, 0, 2, 1, x_t, 1, lora, {0: lambda: turn_logits(sec, 1, 0),
                                                           2: lambda: turn_gates(sec, 1)})

            def hid_ready(sec, kt):
                pe.wait_ge(mm_read, sec.value("mm_read", kt + 1))

            def first_group(sec):
                for i in range(6):
                    for half in range(2):
                        qkv(sec, i, half, 8, 10, (lambda kt: hid_ready(sec, kt)) if i == 0 else None)
                for n in range(8):
                    scores(sec, n, 2)
                    if n == 1:
                        turn_v(sec, 13, 2)

            def body(sec):
                for step in range(12):
                    qkv(sec, step // 2, step % 2, 0, 0)
                    if 1 <= step <= 6:
                        attend(sec, step - 1)
                    if step <= 5:
                        turn_probs(sec, step)
                pe.wait_ge(o_read, sec.value("o_read", 4))
                for i in range(KT):
                    for half in range(2):
                        project(sec, i, 6 + i, 6 + i // 2, heads=range(2 * half, 2 * half + 2))
                        if 6 <= 2 * i + half < 14:
                            scores(sec, 2 * i + half - 6, 0)
                    if i == 0:
                        turn_v(sec, 5, 6)

            def last_group(sec):
                def first_sample(i):
                    project(sec, i, i, i // 2, tokens=slice(0, SEQ))

                turn_probs(sec, 0, two_banks=True)
                turn_probs(sec, 1, two_banks=True)
                for i in range(4):
                    attend(sec, i)
                    turn_probs(sec, i + 2, two_banks=True)
                pe.wait_ge(o_read, sec.value("o_read", 2))
                first_sample(0)
                attend(sec, 4)
                first_sample(1)
                attend(sec, 5)
                for i in range(2, KT):
                    first_sample(i)
                pe.wait_ge(o_read, sec.value("o_read", 4))
                for i in range(KT):
                    project(sec, i, KT + i, i // 2, tokens=slice(SEQ, CHUNK))

            def cond2(sec):
                pe.wait_ge(o_read, sec.value("o_read", 3))
                slot = sec.slot(4)
                tile_ready(sec, 4)
                for kt in range(KT):
                    pe.wait_ge(x1_lo, sec.value("x1_lo", KT + kt + 1))
                    both = w_sb[:, slot, 0, kt * 2 * OWN:kt * 2 * OWN + P]
                    nc.tensor.matmul(ob[:, 0, :], both, hid_src(0, kt), start=kt == 0, stop=False,
                                     skip_group_check=True)
                    last = nc.tensor.matmul(ob[:, 0, :], both, hid_src(1, kt), start=False, stop=kt == KT - 1,
                                            skip_group_check=True)
                last.then_inc(o_ready, 1)
                base_and_lora(sec, 16, 6, 5, hid_src, 1, own_lora, {})

            def ffn(sec):
                pe.wait_ge(o_read, sec.value("o_read", 4))
                linear(sec, ob[:, 1, :], 14, y1, ready=lambda kt: pe.wait_ge(mm_read, sec.value("mm_read", 16 + kt + 1))
                       ).then_inc(o_ready, 1)
                pe.wait_ge(s_read, sec.value("s_read", 0))
                logits(sec, 1, sc[:, 0, :], y1)
                base_and_lora(sec, 24, 16, 15, y1, 2, lora, {0: lambda: turn_logits(sec, 1, 6),
                                                             2: lambda: turn_gates(sec, 7)})

            with pe.Fori(0, CHUNKS) as c:
                pre = Section("pre", c)
                cond(pre)
                first_group(pre)
                with pe.Fori(0, BODIES) as g:
                    body(Section("body", c, g))
                post = Section("post", c)
                last_group(post)
                cond2(post)
                ffn(post)

        @block.scalar
        def _(act):
            def split_hi(sec, tile, dst=None):
                s = sec.slot(tile)
                act.wait_ge(w_raw[s], sec.round(tile) * 16)
                nc.scalar.copy(w_sb[:, s, 0, :] if dst is None else dst, w_raw_sb[:, s, :]).then_inc(w_hi[s], 1)

            def rope_swap(sec, n, k):
                s = n % 2
                act.wait_ge(mm_ready, sec.value("mm_ready", n + 1))
                act.wait_ge(rope_lo, sec.value("rope_lo", (0, 0, 1, 2, 3)[k]))
                nc.scalar.copy(swap[0:P // 2, s, :], mm[P // 2:P, s, :])
                nc.scalar.copy(swap[P // 2:P, s, :], mm[0:P // 2, s, :]).then_inc(xs_ready, 1)

            def write_rope_hi(sec, s, k):
                act.wait_ge(rope_sum, sec.value("rope_sum", k + 1))
                dst = k_t[:, 0, :] if k == 0 else q_t(0, k - 1)
                nc.scalar.copy(dst, turn[:, s, :]).then_inc(rope_hi, 1)

            def probs_hi(sec, i, bank=ptb):
                act.wait_ge(ptb_ready, sec.value("ptb_ready", i + 1))
                nc.scalar.copy(p_t[:, i % 2, 0, :], bank[:]).then_inc(ptb_hi, 1)

            def v_hi(sec, ordinal, k):
                act.wait_ge(ptb_ready, sec.value("ptb_ready", ordinal + 1))
                nc.scalar.copy(v_tok[:, 0, :, :], ptb[:].rearrange("p (t d) -> p t d", t=TT)).then_inc(ptb_hi, 1)

            def write_o_hi(sec, n):
                b, qt = n // QT, n % QT
                act.wait_ge(o_ready, sec.value("o_ready", n + 1))
                t0 = b * SEQ + qt * P
                nc.scalar.copy(wide[:, 2, :, t0:t0 + P], ob[:, qt, :].rearrange("p (h t) -> p h t", h=HG)
                               ).then_inc(o_hi, 1)

            def softmax_exp(sec, n):
                b, qt = n // QT, n % QT
                keys = (qt + 1) * P
                act.wait_ge(nmax_ready, sec.value("nmax_ready", n + 1))
                for h in range(HG):
                    pr = probs[:, b, qt, h, 0:keys]
                    last = nc.scalar.activation(pr, pr, ACT.Exp, bias=nmax[:, n, h:h + 1], scale=SCALE,
                                                accum_out=rowsum[:, n, h:h + 1])
                last.then_inc(exp_ready, 1)

            def split_hg():
                nc.scalar.copy(p_t[:, 0, 0, :], hg).then_inc(hg_hi, 1)

            def stage_x(chunk):
                for kt in range(KT):
                    act.dma_start(staged(kt), x_in[bass.ds(chunk, 1), :, kt, :].rearrange("c p t -> p (c t)")
                                  ).then_inc(x_staged[kt], 16)

            def write_x_hi(chunk, kt):
                act.wait_ge(x_staged[kt], chunk * 16 + 16)
                nc.scalar.copy(x_t(0, kt), staged(kt)).then_inc(x_hi, 1)

            def cond(sec):
                act.wait_ge(out_stored, sec.c * (16 * KT) + 16)
                act.dma_start(acc[:], x_in[bass.ds(sec.c, 1)].rearrange("c p k t -> p (c k) t")
                              ).then_inc(acc_loaded, 16)
                split_hi(sec, 4)
                act.wait_ge(shift_ready, sec.value("shift_ready", 1))
                nc.scalar.activation(expd, shifted, ACT.Exp).then_inc(gate_exp, 1)
                split_hi(sec, 1, lora_b[:, 0, :])
                split_hi(sec, 5)
                act.wait_ge(s_read, sec.value("s_read", 2))
                split_hg()
                for i in range(KT):
                    act.wait_ge(mm_ready, sec.value("mm_ready", i + 1))
                    nc.scalar.copy(hid[:, 0, i, :], lin_bank(i)).then_inc(mm_hi, 1)
                    if i == 0:
                        split_hi(sec, 6)
                    split_hi(sec, 7 + i)

            def first_group(sec):
                rope_swap(sec, 8, 0)
                split_hi(sec, 15)
                write_rope_hi(sec, 0, 0)
                rope_swap(sec, 9, 1)
                split_hi(sec, 16)
                write_rope_hi(sec, 1, 1)
                rope_swap(sec, 10, 2)
                split_hi(sec, 17)
                write_rope_hi(sec, 0, 2)
                rope_swap(sec, 11, 3)
                split_hi(sec, 18)
                write_rope_hi(sec, 1, 3)
                rope_swap(sec, 12, 4)
                split_hi(sec, 19)
                write_rope_hi(sec, 0, 4)
                softmax_exp(sec, 0)
                v_hi(sec, 2, 0)
                softmax_exp(sec, 1)
                softmax_exp(sec, 2)
                softmax_exp(sec, 3)

            def body(sec):
                probs_hi(sec, 0)
                rope_swap(sec, 0, 0)
                probs_hi(sec, 1)
                write_o_hi(sec, 0)
                split_hi(sec, 4)
                probs_hi(sec, 2)
                write_rope_hi(sec, 0, 0)
                rope_swap(sec, 1, 1)
                probs_hi(sec, 3)
                write_o_hi(sec, 1)
                split_hi(sec, 5)
                probs_hi(sec, 4)
                write_o_hi(sec, 2)
                write_rope_hi(sec, 1, 1)
                rope_swap(sec, 2, 2)
                probs_hi(sec, 5)
                split_hi(sec, 6)
                write_o_hi(sec, 3)
                write_rope_hi(sec, 0, 2)
                rope_swap(sec, 3, 3)
                split_hi(sec, 7)
                write_rope_hi(sec, 1, 3)
                rope_swap(sec, 4, 4)
                split_hi(sec, 8)
                write_rope_hi(sec, 0, 4)
                split_hi(sec, 9)
                v_hi(sec, 6, 0)
                act.wait_ge(mm_ready, sec.value("mm_ready", 6))
                split_hi(sec, 10)
                act.wait_ge(mm_ready, sec.value("mm_ready", 8))
                split_hi(sec, 11)
                act.wait_ge(mm_ready, sec.value("mm_ready", 10))
                split_hi(sec, 12)
                softmax_exp(sec, 0)
                softmax_exp(sec, 1)
                softmax_exp(sec, 2)
                act.wait_ge(mm_ready, sec.value("mm_ready", 12))
                split_hi(sec, 13)
                softmax_exp(sec, 3)

            def last_group(sec):
                for i in range(6):
                    probs_hi(sec, i, (ptb, ptb1)[i % 2])
                    if i in (1, 3, 4):
                        write_o_hi(sec, i // 2)
                write_o_hi(sec, 3)
                s = sec.slot(4)
                act.wait_ge(w_raw[s], sec.round(4) * 16)
                nc.scalar.copy(own_a(s, "hi"), own_a(s, "raw")).then_inc(w_hi[s], 1)
                for i in range(KT):
                    act.wait_ge(mm_read, sec.value("mm_read", i + 1))
                    nc.scalar.copy(hid[:, 0, i, 0:SEQ], acc[:, i, 0:SEQ]).then_inc(x1_hi, 1)
                for i in range(KT):
                    act.wait_ge(mm_read, sec.value("mm_read", KT + i + 1))
                    nc.scalar.copy(hid[:, 0, i, SEQ:CHUNK], acc[:, i, SEQ:CHUNK]).then_inc(x1_hi, 1)
                    if i % 2 == 1 and i >= 3:
                        split_hi(sec, 5 + i // 2)

            def cond2(sec):
                stage_x(sec.c + 1)
                s = sec.slot(5)
                act.wait_ge(w_raw[s], sec.round(5) * 16)
                nc.scalar.copy(lora_b[0:3 * OWN, 0, :], w_raw_sb[0:3 * OWN, s, :]).then_inc(w_hi[s], 1)
                act.wait_ge(o_read, sec.value("o_read", 5))
                nc.scalar.copy(p_t[0:OWN, 0, 0, :], hg[0:OWN, :])
                nc.scalar.copy(p_t[2 * OWN:3 * OWN, 0, 0, :], hg[0:OWN, :]).then_inc(hg_hi, 1)
                split_hi(sec, 9)
                for i in range(KT):
                    act.wait_ge(mm_ready, sec.value("mm_ready", 16 + i + 1))
                    nc.scalar.activation(y1(0, i), lin_bank(i), ACT.Identity, bias=bia[:, B_2 + i:B_2 + i + 1]
                                         ).then_inc(mm_hi, 1)
                    if i == 0:
                        split_hi(sec, 10)
                    if i != 4:
                        split_hi(sec, 11 + i)

            def ffn(sec):
                act.wait_ge(shift_ready, sec.value("shift_ready", 1))
                nc.scalar.activation(expd, shifted, ACT.Exp)
                nc.scalar.activation(thr_e, lg.rearrange("p (t e) -> p t e", t=TT)[:, :, E], ACT.Exp,
                                     bias=neg_bthr[:], scale=-1.0).then_inc(gate_exp, 1)
                split_hi(sec, 15, lora_b[:, 0, :])
                act.wait_ge(o_read, sec.value("o_read", 6))
                split_hg()
                split_hi(sec, 19)
                for i in range(KT):
                    act.wait_ge(mm_ready, sec.value("mm_ready", 24 + i + 1))
                    if i == 0:
                        split_hi(sec, 20)
                    if i in AHEAD:
                        split_hi(sec, 21 + i)
                    if 2 <= i < 5:
                        write_x_hi(sec.c + 1, i - 2)
                    if i == KT - 1:
                        write_x_hi(sec.c + 1, 3)
                    act.wait_ge(mm_read, sec.value("mm_read", 24 + i + 1))
                    act.dma_start(out[bass.ds(sec.c, 1), :, i, :].rearrange("c p t -> p (c t)"), acc[:, i, :]
                                  ).then_inc(out_stored, 16)
                for kt in range(4, KT):
                    write_x_hi(sec.c + 1, kt)

            act.sem_inc(out_stored, 16)
            stage_x(0)
            write_x_hi(0, 0)
            split_hi(Section("pre", 0), 0)
            for kt in range(1, KT):
                write_x_hi(0, kt)
            act.wait_ge(gw_loaded, 16)
            nc.scalar.copy(gw[:], gw_raw[:]).then_inc(gw_hi, 1)
            for t in (2, 3):
                split_hi(Section("pre", 0), t)
            act.wait_ge(const_loaded, 16 * N_CONST)
            with act.Fori(0, CHUNKS) as c:
                pre = Section("pre", c)
                cond(pre)
                first_group(pre)
                with act.Fori(0, BODIES) as g:
                    body(Section("body", c, g))
                post = Section("post", c)
                last_group(post)
                cond2(post)
                ffn(post)
            act.wait_ge(out_stored, 16 + CHUNKS * 16 * KT)

        @block.gpsimd
        def _(pool):
            def normalise(sec):
                for n in range(CS * QT):
                    b, qt = n // QT, n % QT
                    pool.wait_ge(rsum_ready, sec.value("rsum_ready", n + 1))
                    pool.sem_inc(passed, 1)
                    for h in range(HG):
                        pr = probs[:, b, qt, h, 0:(qt + 1) * P]
                        last = nc.gpsimd.tensor_scalar(pr, pr, rsum[:, n, h:h + 1], 1.0, ALU.mult, ALU.mult)
                    last.then_inc(p_ready, 1)

            def write_rope_sum(sec, k):
                s = k % 2
                pool.wait_ge(t2_ready, sec.value("t2_ready", k + 1))
                nc.gpsimd.tensor_tensor(turn[:, s, :], turn[:, s, :], swap[:, s, :], ALU.add
                                        ).then_inc(rope_sum, 1)

            with pool.Fori(0, CHUNKS) as c:
                pre = Section("pre", c)
                for k in range(5):
                    write_rope_sum(pre, k)
                normalise(pre)
                with pool.Fori(0, BODIES) as g:
                    sec = Section("body", c, g)
                    for k in range(5):
                        write_rope_sum(sec, k)
                    normalise(sec)

        @block.vector
        def _(dve):
            def split_lo(sec, tile, dst=None):
                s = sec.slot(tile)
                dve.wait_ge(w_hi[s], sec.round(tile))
                hi = w_sb[:, s, 0, :] if dst is None else lora_b[:, 0, :]
                lo = w_sb[:, s, 1, :] if dst is None else lora_b[:, 1, :]
                nc.vector.tensor_tensor(lo, w_raw_sb[:, s, :], f(hi), ALU.subtract).then_inc(w_lo[s], 1)

            def rope_products(sec, n, k):
                s = n % 2
                dve.wait_ge(xs_ready, sec.value("xs_ready", k + 1))
                nc.vector.tensor_tensor(by_sample(turn[:, s, :]), by_sample(mm[:, s, :]), cos, ALU.mult
                                        ).then_inc(mm_read, 1)
                nc.vector.tensor_tensor(by_sample(swap[:, s, :]), by_sample(swap[:, s, :]), sin, ALU.mult
                                        ).then_inc(t2_ready, 1)

            def write_rope_lo(sec, s, k):
                dve.wait_ge(rope_hi, sec.value("rope_hi", k + 1))
                hi, lo = (k_t[:, 0, :], k_t[:, 1, :]) if k == 0 else (q_t(0, k - 1), q_t(1, k - 1))
                nc.vector.tensor_tensor(lo, turn[:, s, :], f(hi), ALU.subtract).then_inc(rope_lo, 1)

            def probs_lo(sec, i, bank=ptb):
                dve.wait_ge(ptb_hi, sec.value("ptb_hi", i + 1))
                nc.vector.tensor_tensor(p_t[:, i % 2, 1, :], bank[:], f(p_t[:, i % 2, 0, :]), ALU.subtract
                                        ).then_inc(ptb_read, 1)

            def v_copy(sec, n):
                dve.wait_ge(mm_ready, sec.value("mm_ready", n + 1))
                nc.vector.tensor_copy(v_raw[:], mm[:, n % 2, :]).then_inc(mm_read, 1)

            def v_lo(sec, k):
                dve.wait_ge(ptb_hi, sec.value("ptb_hi", k))
                four = ptb[:].rearrange("p (t d) -> p t d", t=TT)
                nc.vector.tensor_tensor(v_tok[:, 1, :, :], four, f(v_tok[:, 0, :, :]), ALU.subtract
                                        ).then_inc(ptb_read, 1)

            def write_o_lo(sec, n):
                b, qt = n // QT, n % QT
                t0 = b * SEQ + qt * P
                dve.wait_ge(o_hi, sec.value("o_hi", n + 1))
                nc.vector.tensor_tensor(wide[:, 3, :, t0:t0 + P], ob[:, qt, :].rearrange("p (h t) -> p h t", h=HG),
                                        f(wide[:, 2, :, t0:t0 + P]), ALU.subtract).then_inc(o_read, 1)

            def softmax_max(sec, t, first):
                n, pair = t // 2, t % 2
                b, qt = n // QT, n % QT
                keys = (qt + 1) * P
                mask = cst[:, C_MASK + SEQ - keys:C_MASK + SEQ]
                dve.wait_ge(s_ready, sec.value("s_ready", first + t + 1))
                two = sc[:, t % 2, :].rearrange("p (j hl k) -> p j hl k", j=2, hl=2)
                if qt == 0:
                    nc.vector.tensor_tensor(
                        probs[:, b, 0, 2 * pair:2 * pair + 2, 0:P], two[:, :, 1, :],
                        cst[:, None, C_MASK + P:C_MASK + SEQ].to_broadcast([P, 2, P]), ALU.add).then_inc(low_ready, 1)
                    dve.wait_ge(low_ready, sec.value("low_ready", 2 * b + pair + 1))
                dve.sem_inc(passed, 1)
                for j in range(2):
                    h = 2 * pair + j
                    pr = probs[:, b, qt, h, 0:keys]
                    last = nc.vector.tensor_tensor_reduce(
                        out=pr, in0=sc[:, t % 2, j * SEQ:j * SEQ + keys], in1=pr if qt == 0 else mask,
                        scale=1.0, scalar=-3e38, op0=ALU.add, op1=ALU.max, accum_out=rmax[:, n, h:h + 1])
                last.then_inc(s_read, 1)
                if pair == 1:
                    dve.wait_ge(s_read, sec.value("s_read", first + t + 1))
                    nc.vector.tensor_scalar(nmax[:, n, :], rmax[:, n, :], -SCALE, None, ALU.mult
                                            ).then_inc(nmax_ready, 1)

            def softmax_rsum(sec, n):
                dve.wait_ge(exp_ready, sec.value("exp_ready", n + 1))
                nc.vector.reciprocal(rsum[:, n, :], rowsum[:, n, :]).then_inc(rsum_ready, 1)

            def read_logits(sec, s_ready_k):
                rows = 2 * WG_LO
                dve.wait_ge(s_ready, sec.value("s_ready", s_ready_k))
                nc.vector.tensor_copy(logits_t[0:rows, :], sc[0:rows, 0, :]).then_inc(s_read, 1)

            def read_gates(sec, ordinal):
                dve.wait_ge(ptb_ready, sec.value("ptb_ready", ordinal + 1))
                nc.vector.tensor_copy(gates_t, ptb[:]).then_inc(ptb_read, 1)
                dve.wait_ge(ptb_read, sec.value("ptb_read", ordinal + 1))

            def split_hg(sec, k):
                dve.wait_ge(hg_hi, sec.value("hg_hi", k))
                nc.vector.tensor_tensor(p_t[:, 0, 1, :], hg, f(p_t[:, 0, 0, :]), ALU.subtract
                                        ).then_inc(hg_lo, 1)

            class Steps:

                def __init__(self, sec):
                    self.sec, self.n = sec, 0

                def __call__(self, ins):
                    self.n += 1
                    ins.then_inc(gate_step, 1)
                    dve.wait_ge(gate_step, self.sec.value("gate_step", self.n))

            def turned_logits(n):
                turned = ptb[:, 0:TT * 2 * WG_LO].rearrange("p (t r) -> p t r", t=TT)
                return turned[:, :, 0:n], turned[:, :, WG_LO:WG_LO + n]

            def over_e(ap):
                return ap.rearrange("p (t e) -> p t e", t=TT)

            def per_token(ap):
                return ap[:, :, None].to_broadcast([P, TT, E])

            def spread_gates(step):
                step(nc.vector.scalar_tensor_tensor(out=over_e(gate), in0=over_e(wts), scalar=LORA_SCALE,
                                                    in1=per_token(winv), op0=ALU.mult, op1=ALU.mult))
                nc.vector.tensor_copy(gates_rep.rearrange("p (n r) -> p n r", r=R),
                                      gate[:, :, None].to_broadcast([P, TT * E, R])).then_inc(gates_ready, 1)

            def cond_gates(sec):
                step = Steps(sec)
                lge = over_e(lg[:, 0:TT * E])
                dve.wait_ge(ptb_ready, sec.value("ptb_ready", 1))
                hi_rows, lo_rows = turned_logits(E)
                samples = lang_bias[:, bass.ds(sec.c * CS, CS), :]
                by_sample_too = lambda ap: ap.rearrange("p (s t) e -> p s t e", s=CS)
                step(nc.vector.tensor_tensor(by_sample_too(lge), by_sample_too(lo_rows),
                                             samples[:, :, None, :].to_broadcast([P, CS, QT, E]), ALU.add))
                nc.vector.tensor_tensor(lge, hi_rows, lge, ALU.add).then_inc(ptb_read, 1)
                dve.wait_ge(ptb_read, sec.value("ptb_read", 1))
                step(nc.vector.reduce_max(top, lge, AX))
                nc.vector.tensor_tensor(over_e(shifted), lge, per_token(top), ALU.subtract).then_inc(shift_ready, 1)
                pair = lambda ap: ap.rearrange("p (t e o) -> p t e o", t=TT, e=E)
                other = lge[:, :, None, :].to_broadcast([P, TT, E, E])
                own = lge[:, :, :, None].to_broadcast([P, TT, E, E])
                lower = cst[:, None, C_TRI:C_TRI + E * E].to_broadcast([P, TT, E * E])
                step(nc.vector.tensor_tensor(pair(beats), other, own, ALU.is_gt))
                step(nc.vector.tensor_tensor(pair(ties), other, own, ALU.is_equal))
                flat = lambda ap: ap.rearrange("p (t n) -> p t n", t=TT)
                step(nc.vector.tensor_tensor(flat(ties), flat(ties), lower, ALU.mult))
                step(nc.vector.tensor_tensor(beats, beats, ties, ALU.add))
                step(nc.vector.reduce_sum(rank, beats.rearrange("p (n o) -> p n o", o=E), AX))
                step(nc.vector.tensor_scalar(chosen, rank, 1.5, None, ALU.is_lt))
                dve.wait_ge(gate_exp, sec.value("gate_exp", 1))
                step(nc.vector.tensor_tensor(wts, expd, chosen, ALU.mult))
                step(nc.vector.reduce_sum(wsum, over_e(wts), AX))
                step(nc.vector.reciprocal(winv, wsum))
                spread_gates(step)
                assert step.n == COUNTS["gate_step"][0]

            def ffn_gates(sec):
                step = Steps(sec)
                lg9 = lg.rearrange("p (t e) -> p t e", t=TT)
                dve.wait_ge(ptb_ready, sec.value("ptb_ready", 7))
                hi_rows, lo_rows = turned_logits(E + 1)
                step(nc.vector.tensor_copy(lg9, lo_rows))
                nc.vector.tensor_tensor(lg9, hi_rows, lg9, ALU.add).then_inc(ptb_read, 1)
                dve.wait_ge(ptb_read, sec.value("ptb_read", 7))
                step(nc.vector.reduce_max(top, lg9[:, :, 0:E], AX))
                nc.vector.tensor_tensor(over_e(shifted), lg9[:, :, 0:E], per_token(top), ALU.subtract
                                        ).then_inc(shift_ready, 1)
                dve.wait_ge(gate_exp, sec.value("gate_exp", 1))
                step(nc.vector.reduce_sum(wsum, over_e(expd), AX))
                step(nc.vector.reciprocal(winv, wsum))
                step(nc.vector.tensor_tensor(over_e(rank), over_e(expd), per_token(winv), ALU.mult))
                step(nc.vector.tensor_scalar(thr_1, thr_e, 1.0, None, ALU.add))
                step(nc.vector.reciprocal(thr_r, thr_1))
                step(nc.vector.tensor_scalar(thr, thr_r, MAX_THRESHOLD, None, ALU.mult))
                step(nc.vector.tensor_tensor(over_e(chosen), over_e(rank), per_token(thr), ALU.subtract))
                step(nc.vector.tensor_scalar(wts, chosen, 0.0, None, ALU.max))
                step(nc.vector.reduce_sum(wsum, over_e(wts), AX))
                step(nc.vector.tensor_scalar(is_zero, wsum, 0.0, None, ALU.is_equal))
                step(nc.vector.tensor_tensor(wsum1, wsum, is_zero, ALU.add))
                step(nc.vector.reciprocal(winv, wsum1))
                spread_gates(step)
                assert step.n == COUNTS["gate_step"][2]

            def write_x_lo(count, kt):
                dve.wait_ge(x_hi, count)
                nc.vector.tensor_tensor(x_t(1, kt), staged(kt), f(x_t(0, kt)), ALU.subtract).then_inc(x_lo, 1)

            def cond(sec):
                split_lo(sec, 4)
                read_logits(sec, 2)
                cond_gates(sec)
                split_lo(sec, 1, lora_b)
                split_lo(sec, 5)
                read_gates(sec, 1)
                dve.wait_ge(s_ready, sec.value("s_ready", 1))
                nc.vector.tensor_tensor(hg, sc[:, 1, :], gates_t, ALU.mult).then_inc(s_read, 1)
                split_hg(sec, 1)
                for i in range(KT):
                    dve.wait_ge(mm_hi, sec.value("mm_hi", i + 1))
                    nc.vector.tensor_tensor(hid[:, 1, i, :], lin_bank(i), f(hid[:, 0, i, :]), ALU.subtract
                                            ).then_inc(mm_read, 1)
                    if i == 0:
                        split_lo(sec, 6)
                    split_lo(sec, 7 + i)

            def first_group(sec):
                rope_products(sec, 8, 0)
                split_lo(sec, 15)
                write_rope_lo(sec, 0, 0)
                rope_products(sec, 9, 1)
                split_lo(sec, 16)
                write_rope_lo(sec, 1, 1)
                rope_products(sec, 10, 2)
                split_lo(sec, 17)
                write_rope_lo(sec, 0, 2)
                rope_products(sec, 11, 3)
                split_lo(sec, 18)
                write_rope_lo(sec, 1, 3)
                rope_products(sec, 12, 4)
                split_lo(sec, 19)
                write_rope_lo(sec, 0, 4)
                dve.wait_ge(acc_loaded, sec.c * 16 + 16)
                v_copy(sec, 13)
                softmax_max(sec, 0, 2)
                softmax_max(sec, 1, 2)
                softmax_max(sec, 2, 2)
                softmax_max(sec, 3, 2)
                softmax_rsum(sec, 0)
                softmax_max(sec, 4, 2)
                v_lo(sec, 1)
                softmax_max(sec, 5, 2)
                softmax_max(sec, 6, 2)
                softmax_rsum(sec, 1)
                softmax_max(sec, 7, 2)
                softmax_rsum(sec, 2)
                softmax_rsum(sec, 3)

            def body(sec):
                probs_lo(sec, 0)
                rope_products(sec, 0, 0)
                probs_lo(sec, 1)
                write_o_lo(sec, 0)
                split_lo(sec, 4)
                probs_lo(sec, 2)
                write_rope_lo(sec, 0, 0)
                rope_products(sec, 1, 1)
                probs_lo(sec, 3)
                write_o_lo(sec, 1)
                split_lo(sec, 5)
                probs_lo(sec, 4)
                write_o_lo(sec, 2)
                write_rope_lo(sec, 1, 1)
                rope_products(sec, 2, 2)
                probs_lo(sec, 5)
                split_lo(sec, 6)
                write_o_lo(sec, 3)
                write_rope_lo(sec, 0, 2)
                rope_products(sec, 3, 3)
                split_lo(sec, 7)
                write_rope_lo(sec, 1, 3)
                rope_products(sec, 4, 4)
                split_lo(sec, 8)
                write_rope_lo(sec, 0, 4)
                v_copy(sec, 5)
                split_lo(sec, 9)
                add_projection(sec, 0, 6)
                v_lo(sec, 7)
                split_lo(sec, 10)
                add_projection(sec, 1, 6)
                split_lo(sec, 11)
                add_projection(sec, 2, 6)
                softmax_max(sec, 0, 0)
                add_projection(sec, 3, 6)
                softmax_max(sec, 1, 0)
                split_lo(sec, 12)
                softmax_max(sec, 2, 0)
                add_projection(sec, 4, 6)
                softmax_max(sec, 3, 0)
                softmax_rsum(sec, 0)
                softmax_max(sec, 4, 0)
                add_projection(sec, 5, 6)
                softmax_max(sec, 5, 0)
                softmax_rsum(sec, 1)
                softmax_max(sec, 6, 0)
                add_projection(sec, 6, 6)
                softmax_max(sec, 7, 0)
                softmax_rsum(sec, 2)
                split_lo(sec, 13)
                add_projection(sec, 7, 6)
                softmax_rsum(sec, 3)

            def add_projection(sec, i, first_out, tokens=slice(0, CHUNK)):
                n = first_out + i
                dve.wait_ge(mm_ready, sec.value("mm_ready", n + 1))
                nc.vector.tensor_tensor(acc[:, i, tokens], mm[:, n % 2, tokens], acc[:, i, tokens], ALU.add
                                        ).then_inc(mm_read, 1)

            def last_group(sec):
                for i in range(6):
                    probs_lo(sec, i, (ptb, ptb1)[i % 2])
                    if i in (2, 3, 4):
                        write_o_lo(sec, i - 2)
                add_projection(sec, 0, 0, slice(0, SEQ))
                add_projection(sec, 1, 0, slice(0, SEQ))
                write_o_lo(sec, 3)
                add_projection(sec, 2, 0, slice(0, SEQ))
                s = sec.slot(4)
                dve.wait_ge(w_hi[s], sec.round(4))
                nc.vector.tensor_tensor(own_a(s, "lo"), own_a(s, "raw"), f(own_a(s, "hi")), ALU.subtract
                                        ).then_inc(w_lo[s], 1)
                for i in range(3, KT):
                    add_projection(sec, i, 0, slice(0, SEQ))
                    write_x1_lo(sec, i - 3, 0)
                for i in range(KT - 3, KT):
                    write_x1_lo(sec, i, 0)
                for i in range(KT):
                    add_projection(sec, i, KT, slice(SEQ, CHUNK))
                    if i >= 1:
                        write_x1_lo(sec, i - 1, 1)
                    if i == KT - 1:
                        write_x1_lo(sec, i, 1)
                    if i % 2 == 1 and i >= 3:
                        split_lo(sec, 5 + i // 2)

            def write_x1_lo(sec, i, b):
                tokens = slice(b * SEQ, (b + 1) * SEQ)
                dve.wait_ge(x1_hi, sec.value("x1_hi", b * KT + i + 1))
                nc.vector.tensor_tensor(hid[:, 1, i, tokens], acc[:, i, tokens], f(hid[:, 0, i, tokens]), ALU.subtract
                                        ).then_inc(x1_lo, 1)

            def cond2(sec):
                s = sec.slot(5)
                lo_rows = lora_b[2 * OWN:3 * OWN, 0, :]
                dve.wait_ge(w_hi[s], sec.round(5))
                nc.vector.tensor_tensor(lo_rows, w_raw_sb[2 * OWN:3 * OWN, s, :], f(lo_rows), ALU.subtract
                                        ).then_inc(w_lo[s], 1)
                dve.wait_ge(o_ready, sec.value("o_ready", 5))
                low = gates_t[0:OWN, :]
                for b in range(CS):
                    cols = slice(b * SEQ, (b + 1) * SEQ)
                    last = nc.vector.tensor_scalar(low[:, cols], ob[OWN:2 * OWN, 0, cols],
                                                   cst[OWN:2 * OWN, C_OWN + b:C_OWN + b + 1], None, ALU.mult)
                last.then_inc(own_low, 1)
                dve.wait_ge(own_low, sec.value("own_low", 1))
                for b in range(CS):
                    cols = slice(b * SEQ, (b + 1) * SEQ)
                    last = nc.vector.scalar_tensor_tensor(
                        out=hg[0:OWN, cols], in0=ob[0:OWN, 0, cols], scalar=cst[0:OWN, C_OWN + b:C_OWN + b + 1],
                        in1=low[:, cols], op0=ALU.mult, op1=ALU.add)
                last.then_inc(o_read, 1)
                dve.wait_ge(hg_hi, sec.value("hg_hi", 1))
                nc.vector.tensor_tensor(p_t[OWN:2 * OWN, 0, 0, :], hg[0:OWN, :], f(p_t[0:OWN, 0, 0, :]), ALU.subtract
                                        ).then_inc(hg_lo, 1)
                split_lo(sec, 9)
                for i in range(KT):
                    dve.wait_ge(mm_hi, sec.value("mm_hi", i + 1))
                    nc.vector.scalar_tensor_tensor(out=y1(1, i), in0=lin_bank(i),
                                                   scalar=bia[:, B_2 + i:B_2 + i + 1], in1=f(y1(0, i)),
                                                   op0=ALU.add, op1=ALU.subtract).then_inc(mm_read, 1)
                    if i == 0:
                        split_lo(sec, 10)
                    if i != 4:
                        split_lo(sec, 11 + i)

            def ffn(sec):
                read_logits(sec, 1)
                ffn_gates(sec)
                split_lo(sec, 15, lora_b)
                read_gates(sec, 7)
                dve.wait_ge(o_ready, sec.value("o_ready", 6))
                nc.vector.tensor_tensor(hg, ob[:, 1, :], gates_t, ALU.mult).then_inc(o_read, 1)
                split_hg(sec, 2)
                split_lo(sec, 19)
                for i in range(KT):
                    dve.wait_ge(mm_ready, sec.value("mm_ready", 24 + i + 1))
                    nc.vector.scalar_tensor_tensor(out=acc[:, i, :], in0=lin_bank(i),
                                                   scalar=bia[:, B_B + i:B_B + i + 1], in1=acc[:, i, :],
                                                   op0=ALU.add, op1=ALU.add).then_inc(mm_read, 1)
                    if i == 0:
                        split_lo(sec, 20)
                    if i in AHEAD:
                        split_lo(sec, 21 + i)
                    if 2 <= i < 5:
                        write_x_lo(sec.value("x_hi", i - 1), i - 2)
                for kt in range(3, KT):
                    write_x_lo(sec.value("x_hi", kt + 1), kt)

            done = [0]

            def link(ins):
                done[0] += 1
                ins.then_inc(setup, 1)
                dve.wait_ge(setup, done[0])

            def gate_columns(w, start):
                steps = w[:, :, 0:KT * WG_STEP].rearrange("p w (k n) -> p w k n", k=KT)
                return steps[:, :, :, start:start + WG_LO]

            dve.wait_ge(ids_loaded, 16)
            link(nc.vector.tensor_copy(ids_f[:], ids_raw[:]))
            link(nc.vector.tensor_scalar(slot_neg[:], ids_f[:, 1, :], 0.0, float(SLOTS), ALU.is_lt, ALU.mult))
            link(nc.vector.tensor_tensor(ids_f[:, 1, :], ids_f[:, 1, :], slot_neg[:], ALU.add))
            link(nc.vector.tensor_scalar(slot_neg[:], ids_f[:, 1, :], 0.0, float(SLOTS - 1), ALU.max, ALU.min))
            nc.vector.tensor_copy(slot_ids[:], slot_neg[:]).then_inc(slots_ready, 1)
            write_x_lo(1, 0)
            split_lo(Section("pre", 0), 0)
            for kt in range(1, KT):
                write_x_lo(kt + 1, kt)
            dve.wait_ge(gw_hi, 1)
            nc.vector.tensor_tensor(gate_columns(gw, WG_LO), gate_columns(gw_raw, 0), f(gate_columns(gw, 0)),
                                    ALU.subtract).then_inc(gw_lo, 1)
            for t in (2, 3):
                split_lo(Section("pre", 0), t)
            dve.wait_ge(const_loaded, 16 * N_CONST)
            iota = cst[:, None, C_IOTA:C_IOTA + E].to_broadcast([P, SAMPLES, E])
            lang = ids_f[:, 0, :, None].to_broadcast([P, SAMPLES, E])
            link(nc.vector.tensor_tensor(lang_bias[:], iota, lang, ALU.is_equal))
            link(nc.vector.tensor_scalar(lang_bias[:], lang_bias[:], LANG_BIAS, None, ALU.mult))
            link(nc.vector.tensor_scalar(neg_bthr[:], bia[:, B_THR:B_THR + 1], -1.0, None, ALU.mult))
            with dve.Fori(0, CHUNKS) as c:
                pre = Section("pre", c)
                cond(pre)
                first_group(pre)
                with dve.Fori(0, BODIES) as g:
                    body(Section("body", c, g))
                post = Section("post", c)
                last_group(post)
                cond2(post)
                ffn(post)


def shape_constants():
    f32 = np.float32
    inv_freq = (f32(1.0) / f32(10000.0) ** (np.arange(0, HD, 2, dtype=f32) / f32(HD))).astype(f32)
    freqs = np.outer(np.arange(SEQ, dtype=f32), inv_freq).astype(f32).T
    c = np.zeros((P, C_COLS), f32)
    c[:, C_COS:C_COS + SEQ] = np.concatenate([np.cos(freqs), np.cos(freqs)])
    c[:, C_SIN:C_SIN + SEQ] = np.concatenate([-np.sin(freqs), np.sin(freqs)])
    q, k = np.arange(P)[:, None], np.arange(P)[None, :]
    c[:, C_MASK + P:C_MASK + 2 * P] = np.where(k > q, f32(MASKED), f32(0))
    c[:, C_ID:C_ID + P] = np.eye(P, dtype=f32)
    c[:, C_TRI:C_TRI + E * E] = (np.arange(E)[None, :] < np.arange(E)[:, None]).astype(f32).reshape(1, -1)
    c[:, C_IOTA:C_IOTA + E] = np.arange(E, dtype=f32)
    c[:, C_OWN:C_OWN + CS] = np.where(np.arange(P)[:, None] % OWN // R == np.arange(CS), f32(LORA_SCALE), f32(0))
    return c


def weight_tiles(i):
    def rows(w):
        return w.reshape(-1, P, KT, P).transpose(0, 3, 2, 1).reshape(-1, P, D)

    def lora_a(a):
        return rows(a.reshape(E * R, D))

    def lora_b(b):
        return b.transpose(0, 2, 1).reshape(1, E * R, D)

    wqkv = rows(i["L0_attn_Wqkv"])
    order = [[HEADS + g] + [HG * g + h for h in range(HG)] + [HEADS + KV + g] for g in range(KV)]
    wo = i["L0_attn_Wo"].reshape(KT // 2, 2, P, KV, HG, HD).transpose(3, 0, 5, 1, 4, 2).reshape(KV, KT // 2, P, D)
    parts = [lora_a(i["L0_cond_A"]), lora_b(i["L0_cond_B"]), rows(i["L0_cond_W"]), wqkv[order[0]]]
    for g in range(BODIES):
        parts += [wqkv[order[g + 1]], wo[g]]
    parts += [wo[KV - 1], rows(i["L0_cond2_W"]), lora_a(i["L0_ffn_A_w"]), lora_b(i["L0_ffn_B_w"]),
              rows(i["L0_ffn_W_base"])]
    return np.ascontiguousarray(np.concatenate(parts))


def kernel(**inputs):
    import concourse.bacc as bacc
    from concourse.bass_utils import run_bass_kernel_spmd

    i = {k: np.asarray(v) for k, v in inputs.items()}
    f32 = np.float32
    x = i["x"].reshape(CHUNKS, CHUNK, KT, P).transpose(0, 3, 2, 1)
    x = np.concatenate([x, x[:1]])
    gate_w = np.zeros((P, 2, WG_COLS), f32)
    wr = i["L0_cond_Wr"].reshape(E, KT, P)
    wg = np.concatenate([i["L0_ffn_W_gate"], i["L0_ffn_W_thr"][None]]).reshape(E + 1, KT, P)
    for kt in range(KT):
        gate_w[:, 0, kt * WG_STEP:kt * WG_STEP + E] = wr[:, kt].T
        gate_w[:, 1, kt * WG_STEP:kt * WG_STEP + E + 1] = wg[:, kt].T
    biases = np.concatenate([i["L0_cond2_b"].reshape(KT, P).T, i["L0_ffn_b_base"].reshape(KT, P).T,
                             np.broadcast_to(i["L0_ffn_b_thr"], (P, 1))], axis=1)
    ids = np.broadcast_to(np.stack([i["itok_B_0_7"], i["itok_B_0_23"]]), (P, 2, SAMPLES))
    arrays = {
        "x": x,
        "stream": weight_tiles(i),
        "adapters_a": i["L0_cond2_lora_As"].reshape(SLOTS, KT, P, R).transpose(0, 2, 1, 3),
        "adapters_b": i["L0_cond2_lora_Bs"],
        "gate_w": gate_w,
        "consts": shape_constants(),
        "biases": biases,
        "ids": ids,
    }
    arrays = {k: np.ascontiguousarray(v) for k, v in arrays.items()}
    nc = bacc.Bacc("TRN2", target_bir_lowering=False, num_devices=1)
    args = [nc.dram_tensor(k, a.shape, mybir.dt.from_np(a.dtype), kind="ExternalInput").ap()
            for k, a in arrays.items()]
    out = nc.dram_tensor("out", (CHUNKS, P, KT, CHUNK), F32, kind="ExternalOutput").ap()
    build(nc, *args, out)
    got = run_bass_kernel_spmd(nc, [arrays], core_ids=[0]).results[0]["out"]
    return got.transpose(0, 3, 2, 1).reshape(SAMPLES, SEQ, D)
```
